# Optimizing a Trainium2 kernel written in Bass

```python
import numpy as np
import jax
import jax.numpy as jnp

def _softmax(x, axis=-1):
    return jax.nn.softmax(x, axis=axis)

def _gelu(x):
    return jax.nn.gelu(x, approximate=True)

def _silu(x):
    return jax.nn.silu(x)

def _sigmoid(x):
    return jax.nn.sigmoid(x)

def _layernorm(x, axis=-1, eps=1e-05):
    m = jnp.mean(x, axis=axis, keepdims=True)
    v = jnp.var(x, axis=axis, keepdims=True)
    return (x - m) / jnp.sqrt(v + eps)

def _scatter_add(tgt, idx, src, axis=0):
    return tgt.at[idx].add(src)

def _segment_sum(src, seg, n):
    return jax.ops.segment_sum(src, seg, n)
kernel_name = 'mk_adaln_d1_jaxref_r8_169c91'

def setup_inputs(seed: int=0):
    np.random.seed(seed)
    _w = jnp.asarray

    def _L0_attn_setup():
        import jax, jax.numpy as jnp
        import numpy as np
        D_MODEL = 256
        N_HEADS = 16
        N_KV_HEADS = 4
        HEAD_DIM = D_MODEL // N_HEADS
        ROPE_BASE = 10000.0

        def _rope_tables(T, head_dim):
            half = head_dim // 2
            theta = 1.0 / ROPE_BASE ** (jnp.arange(half, dtype=jnp.float32) / half)
            m = jnp.arange(T, dtype=jnp.float32)
            freqs = jnp.outer(m, theta)
            return (jnp.cos(freqs), jnp.sin(freqs))

        def _apply_rope(x, cos, sin):
            half = x.shape[-1] // 2
            x1, x2 = (x[..., :half], x[..., half:])
            cos = cos[None, None, :, :]
            sin = sin[None, None, :, :]
            return jnp.concatenate([x1 * cos - x2 * sin, x1 * sin + x2 * cos], axis=-1)
        key = jax.random.key(seed)
        ks = jax.random.split(key, 5)
        B, T = (4, 256)
        x = jax.random.normal(ks[0], (B, T, D_MODEL), dtype=jnp.float32)
        Wq = jax.random.normal(ks[1], (D_MODEL, N_HEADS * HEAD_DIM), dtype=jnp.float32) * 0.02
        Wk = jax.random.normal(ks[2], (D_MODEL, N_KV_HEADS * HEAD_DIM), dtype=jnp.float32) * 0.02
        Wv = jax.random.normal(ks[3], (D_MODEL, N_KV_HEADS * HEAD_DIM), dtype=jnp.float32) * 0.02
        Wo = jax.random.normal(ks[4], (N_HEADS * HEAD_DIM, D_MODEL), dtype=jnp.float32) * (0.02 / np.sqrt(2.0))
        return {'x': x, 'Wq': Wq, 'Wk': Wk, 'Wv': Wv, 'Wo': Wo}
    _L0_attn_in = _L0_attn_setup()

    def _L0_ffn_setup():
        import jax, jax.numpy as jnp
        import numpy as np
        H = 256
        E = 8
        K = 2
        I = 16
        key = jax.random.key(seed)
        k1, k2, k3, k4 = jax.random.split(key, 4)
        B, T = (2, 512)
        x = jax.random.normal(k1, (B, T, H), dtype=jnp.float32)
        router_w = jax.random.normal(k2, (E, H), dtype=jnp.float32) / np.sqrt(H)
        down_w = jax.random.normal(k3, (E, I, H), dtype=jnp.float32) / np.sqrt(H)
        up_w = jax.random.normal(k4, (E, H, I), dtype=jnp.float32) / np.sqrt(I)
        return {'x': x, 'router_w': router_w, 'down_w': down_w, 'up_w': up_w}
    _L0_ffn_in = _L0_ffn_setup()
    _L0_c = _w((lambda *s: np.random.randn(*s).astype(np.float32) * 0.05)(2, 256))
    _L0_wmod = _w((lambda *s: np.random.randn(*s).astype(np.float32) * 0.05)(256, 6 * 256) * 256 ** (-0.5))
    _d = {'L0_attn_x': _L0_attn_in['x'], 'L0_attn_Wq': _L0_attn_in['Wq'], 'L0_attn_Wk': _L0_attn_in['Wk'], 'L0_attn_Wv': _L0_attn_in['Wv'], 'L0_attn_Wo': _L0_attn_in['Wo'], 'L0_ffn_router_w': _L0_ffn_in['router_w'], 'L0_ffn_down_w': _L0_ffn_in['down_w'], 'L0_ffn_up_w': _L0_ffn_in['up_w'], 'L0_c': _L0_c, 'L0_wmod': _L0_wmod}
    _x0 = _d['L0_attn_x']
    _d['L0_attn_x'] = jax.random.normal(jax.random.fold_in(jax.random.key(seed), 1), (2, 1024, 256), dtype=_x0.dtype)
    del _x0
    return _d

def reference(L0_attn_x, L0_attn_Wq, L0_attn_Wk, L0_attn_Wv, L0_attn_Wo, L0_ffn_router_w, L0_ffn_down_w, L0_ffn_up_w, L0_c, L0_wmod):

    def _L0_attn_ref(x, Wq, Wk, Wv, Wo):
        import jax, jax.numpy as jnp
        import numpy as np
        D_MODEL = 256
        N_HEADS = 16
        N_KV_HEADS = 4
        HEAD_DIM = D_MODEL // N_HEADS
        ROPE_BASE = 10000.0

        def _rope_tables(T, head_dim):
            half = head_dim // 2
            theta = 1.0 / ROPE_BASE ** (jnp.arange(half, dtype=jnp.float32) / half)
            m = jnp.arange(T, dtype=jnp.float32)
            freqs = jnp.outer(m, theta)
            return (jnp.cos(freqs), jnp.sin(freqs))

        def _apply_rope(x, cos, sin):
            half = x.shape[-1] // 2
            x1, x2 = (x[..., :half], x[..., half:])
            cos = cos[None, None, :, :]
            sin = sin[None, None, :, :]
            return jnp.concatenate([x1 * cos - x2 * sin, x1 * sin + x2 * cos], axis=-1)
        B, T, C = x.shape
        groups = N_HEADS // N_KV_HEADS
        q = (x @ Wq).reshape(B, T, N_HEADS, HEAD_DIM).transpose(0, 2, 1, 3)
        k = (x @ Wk).reshape(B, T, N_KV_HEADS, HEAD_DIM).transpose(0, 2, 1, 3)
        v = (x @ Wv).reshape(B, T, N_KV_HEADS, HEAD_DIM).transpose(0, 2, 1, 3)
        cos, sin = _rope_tables(T, HEAD_DIM)
        q = _apply_rope(q, cos, sin)
        k = _apply_rope(k, cos, sin)
        k = jnp.repeat(k, groups, axis=1)
        v = jnp.repeat(v, groups, axis=1)
        scale = 1.0 / np.sqrt(HEAD_DIM)
        scores = jnp.einsum('bhqd,bhkd->bhqk', q, k) * scale
        pos = jnp.arange(T)
        dist = jnp.minimum(pos[None, :] - pos[:, None], 0).astype(jnp.float32)
        slopes = 2.0 ** (-8.0 * jnp.arange(1, N_HEADS + 1, dtype=jnp.float32) / N_HEADS)
        alibi = slopes[:, None, None] * dist[None, :, :]
        scores = scores + alibi[None]
        causal = pos[None, :] > pos[:, None]
        scores = jnp.where(causal[None, None], -jnp.inf, scores)
        weights = jax.nn.softmax(scores, axis=-1)
        out = jnp.einsum('bhqk,bhkd->bhqd', weights, v)
        out = out.transpose(0, 2, 1, 3).reshape(B, T, N_HEADS * HEAD_DIM)
        return out @ Wo

    def _L0_ffn_ref(x, router_w, down_w, up_w):
        import jax, jax.numpy as jnp
        import numpy as np
        H = 256
        E = 8
        K = 2
        I = 16
        logits = jnp.einsum('bth,eh->bte', x, router_w)
        weights = jax.nn.softmax(logits, axis=-1)
        top_w, top_idx = jax.lax.top_k(weights, K)
        topk_mask = jnp.sum(jax.nn.one_hot(top_idx, E, dtype=x.dtype), axis=-2)
        gate = weights * topk_mask
        h = jnp.einsum('bth,eih->beti', x, down_w)
        a = jax.nn.silu(h)
        expert_out = jnp.einsum('beti,ehi->beth', a, up_w)
        out = jnp.einsum('beth,bte->bth', expert_out, gate)
        return out
    x = L0_attn_x
    mod = (_silu(L0_c) @ L0_wmod).reshape(L0_c.shape[0], 6, 1, -1)
    sa, ca, ga, sb, cb, gb = (mod[:, 0], mod[:, 1], mod[:, 2], mod[:, 3], mod[:, 4], mod[:, 5])
    ga = (2 * (ga >= 0) - 1) * jnp.maximum(jnp.abs(ga), 0.25)
    gb = (2 * (gb >= 0) - 1) * jnp.maximum(jnp.abs(gb), 0.25)
    h = _layernorm(x, axis=-1) * (1 + ca) + sa
    x = x + ga * _L0_attn_ref(h, L0_attn_Wq, L0_attn_Wk, L0_attn_Wv, L0_attn_Wo)
    h = _layernorm(x, axis=-1) * (1 + cb) + sb
    x = x + gb * _L0_ffn_ref(h, L0_ffn_router_w, L0_ffn_down_w, L0_ffn_up_w)
    return x

_drawn_inputs = setup_inputs


def setup_inputs(seed=0):
    import zlib

    import numpy as np

    out = dict(_drawn_inputs(seed))
    spreads = {}
    factors = {'L0_attn_Wq': 8.0, 'L0_attn_Wk': 8.0, 'L0_attn_Wv': 8.0, 'L0_attn_Wo': 8.0}
    for name, (base, spread) in spreads.items():
        noise = np.random.default_rng([zlib.crc32(name.encode()), seed]).standard_normal(out[name].shape)
        drawn = base * np.exp(spread * noise) if base else spread * noise
        out[name] = jnp.asarray(drawn.astype(out[name].dtype))
    for name, factor in factors.items():
        out[name] = (out[name] * factor).astype(out[name].dtype)
    return out
```

```python
from contextlib import ExitStack

import numpy as np

import concourse.bass as bass
from concourse import mybir

F32 = mybir.dt.float32
BF16 = mybir.dt.bfloat16
ALU = mybir.AluOpType
ACT = mybir.ActivationFunctionType
AX = mybir.AxisListType

P = 128
B, T, D = 2, 1024, 256
HEADS, KV_HEADS, HD = 16, 4, 16
GROUP = HEADS // KV_HEADS
NG = B * KV_HEADS
TT = T // P
DC = D // P
QC = HEADS * HD
QK = QC + KV_HEADS * HD
QKV = QK + KV_HEADS * HD
HALF = T // 2
EXPERTS, INNER = 8, 16
EI = EXPERTS * INNER
EPS = 1e-5

FEATURE_ROW = 32
MAX_PARTS = 2
Q_PARTS = (0, 0, 1, 1, 0, 2)
K_PARTS = (0, 1, 0, 1, 2, 0)
MASKED = -1e30

UNITS = 36
P_RING = 18
STEPS = []
_u = 0
for _half in range(2):
    for _kt in range(4 * _half):
        STEPS.append((_half, _u, 4, [(_kt, 0, HALF)], 1))
        _u += 4
    STEPS.append((_half, _u, 4, [(4 * _half, 0, 512)], 1))
    STEPS.append((_half, _u + 4, 4, [(4 * _half + 1, 0, 384), (4 * _half + 3, 384, 128)], 1))
    STEPS.append((_half, _u + 8, 2, [(4 * _half + 2, 0, 256)], 2))
    _u += 10
assert _u == UNITS and P_RING * 2 == UNITS and len(STEPS) == 10
FIRST_STEP = (0, 3)
LAST_STEP = (2, 9)
DIAGONAL = (0, 1, 2, 7, 8, 9)

SLOTS = []
for _t in range(TT):
    _per = {0: 4, 1: 4, 2: 2, 3: 2}.get(_t, 1)
    SLOTS += [(_t, _h, _per) for _h in range(0, GROUP, _per)]
NSLOTS = len(SLOTS)
SLOT_OF_TILE7 = NSLOTS - 4

RING = ([("max", s, 0) for s in range(SLOT_OF_TILE7, NSLOTS)] + [("max", 0, 1), ("max", 1, 1), ("rows", 1, 0)]
        + [("max", s, 1) for s in range(2, 8)] + [("rows", 0, 1)] + [("max", s, 1) for s in range(8, SLOT_OF_TILE7)])
assert len(RING) == NSLOTS + 2 and len(RING) % 2 == 0


def adaln_block(nc, x, w_qkv, w_out, w_hidden_router, w_up, cond_t, w_mod, rope, q_const, k_const,
                causal, ident, rank, out):
    ctx = ExitStack()
    with ctx:
        def sb(name, shape, dt=F32):
            return ctx.enter_context(nc.sbuf_tensor(name, shape, dt))

        def sem(name):
            return ctx.enter_context(nc.semaphore(name))

        q_parts = nc.dram_tensor("q_parts", [3, NG * GROUP * HD, T], BF16, kind="Internal").ap()
        k_parts = nc.dram_tensor("k_parts", [3, NG * HD, T], BF16, kind="Internal").ap()

        x_sb = sb("x_sb", [P, B * TT, D])
        wqkv_sb = sb("wqkv_sb", [P, DC, QKV])
        wo_sb = sb("wo_sb", [P, DC, D])
        whr_sb = sb("whr_sb", [P, DC, EI + EXPERTS])
        up_sb = sb("up_sb", [P, D])
        wmod_sb = sb("wmod_sb", [P, DC, 6 * D])
        cond_sb = sb("cond_sb", [P, DC, B])
        cond_exp = sb("cond_exp", [P, DC, B])
        cond_silu = sb("cond_silu", [P, DC, B])
        cond_rep = sb("cond_rep", [P, DC, B, P])
        mod_cols = sb("mod_cols", [P, 8, B])
        mod_now = sb("mod_now", [P, 8])
        gate_abs = sb("gate_abs", [P, 4, D])
        gates = sb("gates", [P, 4, D])
        wo_gated = sb("wo_gated", [P, B, DC, D])
        up_gated = sb("up_gated", [P, B, D])
        rope_sb = sb("rope_sb", [P, TT, 3, HD // 2])
        causal_sb = sb("causal_sb", [P, P], BF16)
        after_sb = sb("after_sb", [P, P], BF16)
        ident_sb = sb("ident_sb", [P, P])
        ident_bf = sb("ident_bf", [P, P], BF16)
        rank_sb = sb("rank_sb", [P, EXPERTS])
        stats = sb("stats", [P, TT, 6])
        mean_var = sb("mean_var", [P, TT, 2])
        var_eps = sb("var_eps", [P, TT])
        std = sb("std", [P, TT])
        rstd = sb("rstd", [P, TT])
        normed = sb("normed", [P, TT, D])
        h_t = sb("h_t", [P, DC, T])
        v_all = sb("v_all", [P, B, KV_HEADS, TT, 32])
        v_now = sb("v_now", [P, 2, TT, 32])
        k_stack = [sb(f"k_stack{i}", [P, T], BF16) for i in range(2)]
        q_stack = [sb(f"q_stack{i}", [P, GROUP, T], BF16) for i in range(2)]
        probs = sb("probs", [P, P_RING, 512])
        rot_a = probs[:, 0:3, :].rearrange("p a b -> p (a b)")[:, 0:4 * QK].rearrange("p (t c) -> p t c", t=4)
        rot_b = probs[:, 3:6, :].rearrange("p a b -> p (a b)")[:, 0:4 * QK].rearrange("p (t c) -> p t c", t=4)
        rest = probs[:, 6:9, :].rearrange("p a b -> p (a b)")[:, 0:4 * QK].rearrange("p (t c) -> p t c", t=4)
        parts_sb = sb("parts_sb", [P, 2, 3, 4, QK], BF16)
        parts_t = sb("parts_t", [P, 2, 9, 512], BF16)
        neg_max = sb("neg_max", [P, TT, GROUP])
        max_parts = sb("max_parts", [P, TT, GROUP, MAX_PARTS], BF16)
        max_rows = sb("max_rows", [MAX_PARTS * GROUP, T], BF16)
        o_t = sb("o_t", [P, 512])
        inv_sum = sb("inv_sum", [P, 4, GROUP])
        heads_out = sb("heads_out", [P, NG, TT, GROUP * HD])
        o_now = sb("o_now", [P, TT, KV_HEADS, GROUP * HD])
        o_now_t = sb("o_now_t", [P, DC, T])
        x1 = probs[:, 0:4, :].rearrange("p a (b c) -> p (a b) c", c=D)
        logits = sb("logits", [P, TT, EXPERTS])
        router_w = sb("router_w", [P, TT, EXPERTS])
        pick = [sb(f"pick{i}", [P, TT, EXPERTS]) for i in range(5)]
        row_stat = sb("row_stat", [P, 6, TT])
        act = probs[:, 8:10, :].rearrange("p a (b c) -> p (a b) c", c=EI)
        act_exp = probs[:, 10:12, :].rearrange("p a (b c) -> p (a b) c", c=EI)
        act_t = probs[:, 12:14, :]
        y_sb = probs[:, 4:8, :].rearrange("p a (b c) -> p (a b) c", c=D)

        slot_ps = ctx.enter_context(nc.psum_tensor("slot_ps", [P, 2, 1024], F32))
        unit_ps = ctx.enter_context(nc.psum_tensor("unit_ps", [P, 3, 512], F32))
        out_ps = ctx.enter_context(nc.psum_tensor("out_ps", [P, 512], F32))

        in_x, in_w, in_c = sem("in_x"), sem("in_w"), sem("in_c")
        cond_e, cond_s, cond_r = sem("cond_e"), sem("cond_s"), sem("cond_r")
        mod_mm, mod_own, mod_ready = sem("mod_mm"), sem("mod_own"), sem("mod_ready")
        v_zero, v_ones = sem("v_zero"), sem("v_ones")
        ln_own, ln_var, ln_std, ln_x = sem("ln_own"), sem("ln_var"), sem("ln_std"), sem("ln_x")
        now_mod = sem("now_mod")
        x_t, h_ready = sem("x_t"), sem("h_ready")
        qkv_mm, rot_read, v_read, rot_sum = sem("qkv_mm"), sem("rot_read"), sem("v_read"), sem("rot_sum")
        p_hi, p_rest, p_mid, p_lo = sem("p_hi"), sem("p_rest"), sem("p_mid"), sem("p_lo")
        parts_mm, parts_out, parts_dma = sem("parts_mm"), sem("parts_out"), sem("parts_dma")
        ld_q0, ld_k0, ld_hi = ([sem(f"{name}{par}") for par in range(2)] for name in ("ld_q0_", "ld_k0_", "ld_hi_"))
        slot_mm, slot_max = sem("slot_mm"), sem("slot_max")
        hi_own, max_split, rows_mm, rows_out, rows_in = (sem("hi_own"), sem("max_split"), sem("rows_mm"),
                                                         sem("rows_out"), sem("rows_in"))
        unit_mm, unit_exp, v_here = sem("unit_mm"), sem("unit_exp"), sem("v_here")
        pv_mm, o_copied, o_turned, o_inv, o_normed = (sem("pv_mm"), sem("o_copied"), sem("o_turned"),
                                                      sem("o_inv"), sem("o_normed"))
        e_gather, e_tr, e_trout = sem("e_gather"), sem("e_tr"), sem("e_trout")
        yf_mm, yf_used = sem("yf_mm"), sem("yf_used")
        e_x1, e_var, e_std, e_own, e_norm = sem("e_x1"), sem("e_var"), sem("e_std"), sem("e_own"), sem("e_norm")
        hid_mm, hid_exp, hid_used = sem("hid_mm"), sem("hid_exp"), sem("hid_used")
        e_chain, z_ready, z_exp, act_gated = sem("e_chain"), sem("z_ready"), sem("z_exp"), sem("act_gated")
        at_mm, at_out, y_out = sem("at_mm"), sem("at_out"), sem("y_out")

        passed = sem("passed")

        block = ctx.enter_context(nc.Block())

        def settled(eng, semaphore, value):
            eng.wait_ge(semaphore, value)
            eng.sem_inc(passed, 1)

        LD_Q0 = 16 * 7
        LD_K0 = 16 * 6
        LD_HI = 16 * 13
        ROWS_IN = 16 * GROUP

        def load_q(sp, group, par, half, done):
            cols = slice(half * HALF, (half + 1) * HALF)
            sp.dma_start(q_stack[par][0:FEATURE_ROW, :, cols], q_const[group, :, :, cols]).then_inc(done, 16)
            rows = GROUP * HD
            for j, part in enumerate(Q_PARTS):
                lo = FEATURE_ROW + HD * j
                src = q_parts[part, bass.ds(group * rows, rows), cols].rearrange("(h d) t -> d h t", d=HD)
                sp.dma_start(q_stack[par][lo:lo + HD, :, cols], src).then_inc(done, 16)

        def load_k(sp, group, par, half, done):
            cols = slice(half * HALF, (half + 1) * HALF)
            for j, part in enumerate(K_PARTS):
                lo = FEATURE_ROW + HD * j
                sp.dma_start(k_stack[par][lo:lo + HD, cols],
                             k_parts[part, bass.ds(group * HD, HD), cols]).then_inc(done, 16)

        def ahead_of(group, ahead):
            return group + ahead

        @block.sync
        def _(sp):
            sp.dma_start(cond_sb[:], cond_t.rearrange("(k p) b -> p k b", p=P)).then_inc(in_c, 16)
            sp.dma_start(ident_sb[:], ident).then_inc(in_c, 16)
            sp.dma_start(x_sb[:, 0:TT, :], x[0].rearrange("(t p) d -> p t d", p=P)).then_inc(in_x, 16)
            sp.dma_start(wmod_sb[:], w_mod.rearrange("(k p) n -> p k n", p=P)).then_inc(in_c, 16)
            sp.dma_start(wqkv_sb[:], w_qkv.rearrange("(k p) n -> p k n", p=P)).then_inc(in_w, 16)
            sp.dma_start(rope_sb[:], rope).then_inc(in_c, 16)
            sp.dma_start(causal_sb[:], causal[0]).then_inc(in_c, 16)
            sp.dma_start(after_sb[:], causal[1]).then_inc(in_c, 16)
            sp.dma_start(rank_sb[:], rank).then_inc(in_c, 16)
            sp.dma_start(wo_sb[:], w_out.rearrange("(k p) n -> p k n", p=P)).then_inc(in_w, 16)
            sp.dma_start(up_sb[:], w_up).then_inc(in_w, 16)
            sp.dma_start(x_sb[:, TT:2 * TT, :], x[1].rearrange("(t p) d -> p t d", p=P)).then_inc(in_x, 16)
            sp.dma_start(whr_sb[:], w_hidden_router.rearrange("(k p) n -> p k n", p=P)).then_inc(in_w, 16)
            for par in range(2):
                sp.dma_start(k_stack[par][0:FEATURE_ROW, :], k_const).then_inc(in_w, 16)

            with sp.Fori(0, B) as b:
                for k in range(2):
                    cols = slice(k * 512, (k + 1) * 512)
                    for part in range(3):
                        sp.wait_ge(parts_out, b * 10 + 5 * k + part + 1)
                        dst = q_parts[part, bass.ds(b * D, D), cols].rearrange("(c p) t -> p c t", p=P)
                        sp.dma_start(dst, parts_t[:, k, 2 * part:2 * part + 2, :]).then_inc(parts_dma, 16)
                    sp.wait_ge(parts_out, b * 10 + 5 * k + 5)
                    dst = k_parts[:, bass.ds(b * 64, 64), cols].rearrange("a p t -> p a t")
                    sp.dma_start(dst, parts_t[0:64, k, 6:9, :]).then_inc(parts_dma, 16)

            sp.wait_ge(parts_dma, 16 * 16)
            for g in range(2):
                load_q(sp, g, g, 0, ld_q0[g])
                load_k(sp, g, g, 0, ld_k0[g])
                load_q(sp, g, g, 1, ld_hi[g])
                load_k(sp, g, g, 1, ld_hi[g])

            def move_rows(group, par, half, index):
                cols = slice(half * HALF, (half + 1) * HALF)
                sp.wait_ge(rows_out, index + 1)
                for head in range(GROUP):
                    sp.dma_start(q_stack[par][0:MAX_PARTS, head, cols],
                                 max_rows[MAX_PARTS * head:MAX_PARTS * (head + 1), cols]).then_inc(rows_in, 16)

            def attend(n, par, more, load):
                move_rows(n, par, 1, n * 2 + 1)
                if load:
                    sp.wait_ge(unit_mm, n * UNITS + 10)
                    load_q(sp, n + 2, par, 0, ld_q0[par])
                if more:
                    move_rows(n + 1, 1 - par, 0, n * 2 + 2)
                if load:
                    sp.wait_ge(unit_mm, n * UNITS + 26)
                    load_k(sp, n + 2, par, 0, ld_k0[par])
                    sp.wait_ge(unit_mm, n * UNITS + UNITS)
                    load_q(sp, n + 2, par, 1, ld_hi[par])
                    load_k(sp, n + 2, par, 1, ld_hi[par])

            move_rows(0, 0, 0, 0)
            attend(0, 0, True, True)
            with sp.Fori(0, 2) as i:
                attend(i * 2 + 1, 1, True, True)
                attend(i * 2 + 2, 0, True, True)
            attend(5, 1, True, True)
            attend(6, 0, True, False)
            attend(7, 1, False, False)

            with sp.Fori(0, B) as b:
                for t in range(TT):
                    sp.wait_ge(yf_used, b * 16 + TT + t + 1)
                    dst = out[bass.ds(b, 1), t * P:(t + 1) * P, :].rearrange("a p d -> p (a d)")
                    sp.dma_start(dst, y_sb[:, t, :]).then_inc(y_out, 16)
            sp.wait_ge(y_out, 16 * B * TT)

        @block.tensor
        def _(pe):
            pe.wait_ge(in_c, 16 * 7)
            pe.wait_ge(cond_r, 4)
            for j, first in enumerate((0, P, D, D + P, 3 * D, 3 * D + P, 4 * D, 4 * D + P)):
                for k in range(DC):
                    mm = nc.tensor.matmul(out_ps[:, 2 * j:2 * j + 2], wmod_sb[:, k, first:first + P],
                                          cond_silu[:, k, :], start=(k == 0), stop=(k == DC - 1))
            mm.then_inc(mod_mm, 1)
            for j, (first, b) in enumerate(((2 * D, 0), (2 * D, 1), (5 * D, 0), (5 * D, 1))):
                for k in range(DC):
                    mm = nc.tensor.matmul(slot_ps[:, 0, j * D:(j + 1) * D], cond_rep[:, k, b, :],
                                          wmod_sb[:, k, first:first + D], start=(k == 0), stop=(k == DC - 1))
            mm.then_inc(mod_mm, 1)
            pe.wait_ge(in_w, 16 * 6)
            pe.wait_ge(mod_ready, 1)

            def turn_tiles(k, first, tile_done, evac_done, evac_before, tr):
                pe.wait_ge(tile_done[0], tile_done[1])
                if evac_before is not None:
                    pe.wait_ge(evac_done, evac_before)
                for c in range(DC):
                    for t in range(4):
                        mm = nc.tensor.transpose(slot_ps[:, 0, c * 512 + t * P:c * 512 + (t + 1) * P],
                                                 first[:, 4 * k + t, c * P:(c + 1) * P], ident_sb[:])
                    mm.then_inc(tr, 1)

            with pe.Fori(0, B) as b:
                for k in range(2):
                    turn_tiles(k, normed, (ln_x, b * TT + 4 * k + 4), h_ready, b * 4 + 2 * k, x_t)
                    pe.wait_ge(h_ready, b * 4 + 2 * k + 2)
                    for t in range(4):
                        pe.wait_ge(rot_read, b * TT + 4 * k + t)
                        pe.wait_ge(v_read, b * TT + 4 * k + t)
                        for c in range(DC):
                            tok = slice((4 * k + t) * P, (4 * k + t + 1) * P)
                            mm = nc.tensor.matmul(unit_ps[:, t % 2, 0:QKV], h_t[:, c, tok], wqkv_sb[:, c, :],
                                                  start=(c == 0), stop=(c == DC - 1))
                        mm.then_inc(qkv_mm, 1)
                for k in range(2):
                    pe.wait_ge(p_lo, b * 2 + k + 1)
                    for fill in range(5):
                        settled(pe, parts_out, b * 10 + 5 * k + fill)
                        bank = slot_ps[:, 1, (fill % 2) * 512:(fill % 2 + 1) * 512].bitcast(BF16)
                        for s in range(2 if fill < 4 else 1):
                            for t in range(4):
                                col = slice(s * 512 + t * P, s * 512 + (t + 1) * P)
                                if fill < 3:
                                    mm = nc.tensor.transpose(bank[:, col], parts_sb[:, k, fill, t, s * P:(s + 1) * P],
                                                             ident_bf[:])
                                else:
                                    part = 2 * (fill - 3) + s
                                    mm = nc.tensor.transpose(bank[0:64, col], parts_sb[:, k, part, t, QC:QK],
                                                             ident_bf[:])
                        mm.then_inc(parts_mm, 1)

            def slot_count(n, slot):
                return n * NSLOTS + slot + 1

            def ring_event(n, par, where, opening=False):
                kind, which, ahead = RING[where]
                m, mp = (n + ahead if not opening else 0), (par + ahead) % 2
                before = where - 2
                if isinstance(n, int) and n == NG - 1 and kind == "rows":
                    before = None
                if opening:
                    before = {4: None, 5: None, 7: 5, 8: 4}.get(where, before)
                if before is not None:
                    b_kind, b_which, b_ahead = RING[before % len(RING)]
                    if before < 0:
                        b_ahead -= 1
                    of = (n + b_ahead) if not opening else 0
                    if b_kind == "max":
                        if not (isinstance(of, int) and of < 0):
                            pe.wait_ge(slot_max, slot_count(of, b_which))
                    else:
                        pe.wait_ge(rows_out, of * 2 + b_which + 1)
                ps = slot_ps[:, where % 2, :]
                if kind == "rows":
                    pe.wait_ge(max_split, m * 2 + which + 1)
                    bank = ps[:, 0:512].bitcast(BF16)
                    for t in range(4):
                        tile = 4 * which + t
                        mm = nc.tensor.transpose(
                            bank[0:MAX_PARTS * GROUP, t * P:(t + 1) * P],
                            max_parts[:, tile, :, :].rearrange("p h a -> p (h a)"), ident_bf[:])
                    mm.then_inc(rows_mm, 1)
                    return
                tile, head, heads = SLOTS[which]
                if which == 0:
                    pe.wait_ge(ld_q0[mp], m // 2 * LD_Q0 + LD_Q0)
                    pe.wait_ge(ld_k0[mp], m // 2 * LD_K0 + LD_K0)
                if tile == 4 and head == 0:
                    pe.wait_ge(ld_hi[mp], m // 2 * LD_HI + LD_HI)
                keys = (tile + 1) * P
                stride = 1024 // heads
                for j in range(heads):
                    lhs = q_stack[mp][:, head + j, tile * P:(tile + 1) * P]
                    base = j * stride
                    for lo in range(0, keys, 512):
                        hi = min(keys, lo + 512)
                        opens = (base + lo) % 512 == 0
                        mm = nc.tensor.matmul(ps[:, base + lo:base + hi], lhs, k_stack[mp][:, lo:hi],
                                              start=opens, stop=False, skip_group_check=True)
                for j in range(heads):
                    end = j * stride + keys
                    mm = nc.tensor.matmul(ps[:, end - P:end], ident_bf[:], causal_sb[:], start=False, stop=True,
                                          skip_group_check=True)
                mm.then_inc(slot_mm, 1)

            def scores(n, par, step, events):
                half, first, units, blocks, per = STEPS[step]
                if step in FIRST_STEP:
                    pe.wait_ge(rows_in, (n * 2 + half) * ROWS_IN + ROWS_IN)
                for j in range(units):
                    u = first + j
                    if u >= 3 or not (isinstance(n, int) and n == 0):
                        pe.wait_ge(unit_exp, n * UNITS + u - 2)
                    ps = unit_ps[:, u % 3, :]
                    for q in range(per):
                        head = j * per + q
                        for kt, col, width in blocks:
                            at = col + q * width
                            q_lo = max(half * HALF, kt * P)
                            mm = nc.tensor.matmul(ps[:, at:at + width], k_stack[par][:, kt * P:(kt + 1) * P],
                                                  q_stack[par][:, head, q_lo:q_lo + width],
                                                  start=(at == 0), stop=(step not in DIAGONAL),
                                                  skip_group_check=True)
                            if step in DIAGONAL:
                                mm = nc.tensor.matmul(ps[:, at:at + P], ident_bf[:], after_sb[:], start=False,
                                                      stop=True, skip_group_check=True)
                    mm.then_inc(unit_mm, 1)
                    if j < len(events):
                        ring_event(n, par, events[j])
                for e in events[units:]:
                    ring_event(n, par, e)

            def weigh(n, par, step):
                half, first, units, blocks, per = STEPS[step]
                if step == 0:
                    pe.wait_ge(v_here, n + 1)
                if step in FIRST_STEP and not (isinstance(n, int) and n == 0 and step == 0):
                    pe.wait_ge(o_normed, n * 2 + half)
                pe.wait_ge(unit_exp, n * UNITS + first + units)
                for kt, col, width in blocks:
                    q_lo = max(half * HALF, kt * P) - half * HALF
                    for head in range(GROUP):
                        ring = (first + head // per) % P_RING
                        at = col + (head % per) * width
                        mm = nc.tensor.matmul(out_ps[32 * head:32 * head + 32, q_lo:q_lo + width],
                                              v_now[:, par, kt, :], probs[:, ring, at:at + width],
                                              start=(step in FIRST_STEP), stop=(step in LAST_STEP),
                                              skip_group_check=True)
                mm.then_inc(pv_mm, 1)

            def turn_out(n, half):
                pe.wait_ge(o_copied, n * 2 + half + 1)
                for t in range(4):
                    mm = nc.tensor.transpose(out_ps[:, t * P:(t + 1) * P], o_t[:, t * P:(t + 1) * P], ident_sb[:])
                mm.then_inc(o_turned, 1)

            def attend(n, par, first=False, last=False):
                def ev(*which):
                    return [w for w in which if not (last and RING[w][2] == 1)]
                scores(n, par, 0, ev(0, 1, 2, 3))
                if not first:
                    weigh(n - 1, 1 - par, 9)
                scores(n, par, 1, ev(4))
                if not first:
                    turn_out(n - 1, 1)
                scores(n, par, 2, ev(5))
                weigh(n, par, 0)
                ring_event(n, par, 6)
                for w in ev(7):
                    ring_event(n, par, w)
                weigh(n, par, 1)
                for w in ev(8):
                    ring_event(n, par, w)
                weigh(n, par, 2)
                scores(n, par, 3, ev(9, 10))
                turn_out(n, 0)
                scores(n, par, 4, ev(11, 12, 13))
                weigh(n, par, 3)
                scores(n, par, 5, ev(14, 15, 16))
                weigh(n, par, 4)
                scores(n, par, 6, ev(17, 18))
                weigh(n, par, 5)
                scores(n, par, 7, ev(19, 20))
                weigh(n, par, 6)
                scores(n, par, 8, ev(21, 22))
                weigh(n, par, 7)
                scores(n, par, 9, ev(23))
                weigh(n, par, 8)

            for w in (4, 5, *range(7, len(RING))):
                ring_event(-1, 1, w, opening=True)
            attend(0, 0, first=True)
            with pe.Fori(0, 3) as i:
                attend(i * 2 + 1, 1)
                attend(i * 2 + 2, 0)
            attend(7, 1, last=True)
            weigh(7, 1, 9)
            turn_out(7, 1)

            pe.wait_ge(o_normed, NG * 2)
            with pe.Fori(0, B) as b:
                for k in range(2):
                    pe.wait_ge(e_gather, b + 1)
                    pe.wait_ge(e_trout, b * 8 + 2 * k)
                    for c in range(DC):
                        for t in range(4):
                            mm = nc.tensor.transpose(
                                slot_ps[:, 0, c * 512 + t * P:c * 512 + (t + 1) * P],
                                o_now[:, 4 * k + t, 2 * c:2 * c + 2, :].rearrange("p g d -> p (g d)"), ident_sb[:])
                        mm.then_inc(e_tr, 1)
                for t in range(TT):
                    pe.wait_ge(e_trout, b * 8 + 2 * (t // 4) + 2)
                    pe.wait_ge(yf_used, b * 16 + t)
                    for c in range(DC):
                        mm = nc.tensor.matmul(unit_ps[:, t % 2, 0:D], o_now_t[:, c, t * P:(t + 1) * P],
                                              wo_gated[:, b, c, :], start=(c == 0), stop=(c == DC - 1))
                    mm.then_inc(yf_mm, 1)
                for k in range(2):
                    turn_tiles(k, normed, (e_norm, b * TT + 4 * k + 4), e_trout, b * 8 + 4 + 2 * k, e_tr)
                for k in range(2):
                    pe.wait_ge(e_trout, b * 8 + 4 + 2 * k + 2)
                    pe.wait_ge(hid_used, b * 2 + k)
                    for t in range(4):
                        for c in range(DC):
                            tok = slice((4 * k + t) * P, (4 * k + t + 1) * P)
                            mm = nc.tensor.matmul(slot_ps[:, 1, t * 256:t * 256 + EI + EXPERTS], h_t[:, c, tok],
                                                  whr_sb[:, c, :], start=(c == 0), stop=(c == DC - 1),
                                                  skip_group_check=True)
                    mm.then_inc(hid_mm, 1)
                for k in range(2):
                    pe.wait_ge(act_gated, b * 2 + k + 1)
                    pe.wait_ge(at_out, b * 2 + k)
                    for t in range(4):
                        mm = nc.tensor.transpose(unit_ps[:, 2, t * P:(t + 1) * P], act[:, 4 * k + t, :], ident_sb[:])
                    mm.then_inc(at_mm, 1)
                    pe.wait_ge(at_out, b * 2 + k + 1)
                    for t in range(4):
                        pe.wait_ge(yf_used, b * 16 + TT + 4 * k + t)
                        nc.tensor.matmul(unit_ps[:, t % 2, 0:D], act_t[:, k, t * P:(t + 1) * P],
                                         up_gated[:, b, :], start=True, stop=True).then_inc(yf_mm, 1)

        @block.scalar
        def _(act_e):
            act_e.wait_ge(in_c, 16 * 7)
            nc.scalar.activation(cond_exp[:], cond_sb[:], ACT.Exp, scale=-1.0).then_inc(cond_e, 1)
            nc.scalar.copy(ident_bf[:], ident_sb[:]).then_inc(cond_r, 1)
            act_e.wait_ge(mod_mm, 1)
            nc.scalar.copy(mod_cols[:].rearrange("p a b -> p (a b)"), out_ps[:, 0:16]).then_inc(mod_own, 1)
            act_e.wait_ge(v_zero, 1)

            def modulate(k, shift, wait_sem, wait_value, done):
                for c in range(DC):
                    act_e.wait_ge(wait_sem, wait_value + c)
                    nc.scalar.activation(h_t[:, c, k * 512:(k + 1) * 512], slot_ps[:, 0, c * 512:(c + 1) * 512],
                                         ACT.Identity, bias=mod_now[:, shift + c:shift + c + 1],
                                         scale=mod_now[:, shift + 2 + c:shift + 3 + c]).then_inc(done, 1)

            with act_e.Fori(0, B) as b:
                act_e.wait_ge(ln_var, b + 1)
                nc.scalar.activation(std[:], var_eps[:], ACT.Sqrt).then_inc(ln_std, 1)
                for k in range(2):
                    act_e.wait_ge(now_mod, b + 1)
                    modulate(k, 0, x_t, b * 4 + 2 * k + 1, h_ready)
                    for t in range(4):
                        settled(act_e, rot_read, b * TT + 4 * k + t + 1)
                        nc.scalar.copy(v_all[:, b, :, 4 * k + t, 0:HD],
                                       unit_ps[:, t % 2, QK:QKV].rearrange("p (g d) -> p g d", g=KV_HEADS)
                                       ).then_inc(v_read, 1)
                    act_e.wait_ge(rot_sum, b * 2 + k + 1)
                    nc.scalar.copy(parts_sb[:, k, 0, :, :], rot_a).then_inc(p_hi, 1)
                    act_e.wait_ge(p_rest, b * 2 + k + 1)
                    nc.scalar.copy(parts_sb[:, k, 1, :, :], rest).then_inc(p_mid, 1)
                for k in range(2):
                    for fill in range(5):
                        if fill == 0:
                            act_e.wait_ge(parts_dma, b * 128 + 0)
                        act_e.wait_ge(parts_mm, b * 10 + 5 * k + fill + 1)
                        bank = slot_ps[:, 1, (fill % 2) * 512:(fill % 2 + 1) * 512].bitcast(BF16)
                        if fill < 3:
                            dst, src = parts_t[:, k, 2 * fill:2 * fill + 2, :], bank.rearrange("p (s t) -> p s t", s=2)
                        elif fill == 3:
                            dst, src = parts_t[0:64, k, 6:8, :], bank[0:64, :].rearrange("p (s t) -> p s t", s=2)
                        else:
                            dst, src = parts_t[0:64, k, 8, :], bank[0:64, 0:512]
                        nc.scalar.copy(dst, src).then_inc(parts_out, 1)

            def exps(n, step, lo, hi):
                half, first, units, _, _ = STEPS[step]
                for u in range(first + lo, first + hi):
                    user = u - P_RING
                    steps_before = sum(s[1] <= user % UNITS for s in STEPS)
                    if user >= 0:
                        act_e.wait_ge(pv_mm, n * 10 + steps_before)
                    elif not (isinstance(n, int) and n == 0):
                        act_e.wait_ge(pv_mm, n * 10 - 10 + steps_before)
                    act_e.wait_ge(unit_mm, n * UNITS + u + 1)
                    nc.scalar.activation(probs[:, u % P_RING, :], unit_ps[:, u % 3, :], ACT.Exp).then_inc(unit_exp, 1)

            def rows_copy(index, half, where):
                act_e.wait_ge(rows_mm, index + 1)
                if not (isinstance(index, int) and index < 2):
                    act_e.wait_ge(rows_in, index * ROWS_IN - ROWS_IN)
                nc.scalar.copy(max_rows[:, half * HALF:(half + 1) * HALF],
                               slot_ps[0:MAX_PARTS * GROUP, where % 2, 0:512].bitcast(BF16)[:, 0:512]
                               ).then_inc(rows_out, 1)

            def out_copy(n, half):
                act_e.wait_ge(pv_mm, n * 10 + LAST_STEP[half] + 1)
                if not (isinstance(n, int) and n == 0 and half == 0):
                    act_e.wait_ge(o_turned, n * 2 + half)
                nc.scalar.copy(o_t[:], out_ps[:]).then_inc(o_copied, 1)

            def attend(n, first=False, last=False):
                exps(n, 0, 0, 4)
                exps(n, 1, 0, 2)
                if not first:
                    out_copy(n - 1, 1)
                exps(n, 1, 2, 4)
                exps(n, 2, 0, 2)
                rows_copy(n * 2 + 1, 1, 6)
                exps(n, 3, 0, 2)
                out_copy(n, 0)
                exps(n, 3, 2, 4)
                exps(n, 4, 0, 4)
                if not last:
                    rows_copy(n * 2 + 2, 0, 13)
                for step in range(5, 10):
                    exps(n, step, 0, STEPS[step][2])

            rows_copy(0, 0, 13)
            attend(0, first=True)
            with act_e.Fori(0, 3) as i:
                attend(i * 2 + 1)
                attend(i * 2 + 2)
            attend(7, last=True)
            out_copy(7, 1)

            with act_e.Fori(0, B) as b:
                for k in range(2):
                    for c in range(DC):
                        act_e.wait_ge(e_tr, b * 8 + 2 * k + c + 1)
                        nc.scalar.copy(o_now_t[:, c, k * 512:(k + 1) * 512],
                                       slot_ps[:, 0, c * 512:(c + 1) * 512]).then_inc(e_trout, 1)
                act_e.wait_ge(e_var, b + 1)
                nc.scalar.activation(std[:], var_eps[:], ACT.Sqrt).then_inc(e_std, 1)
                for k in range(2):
                    modulate(k, 4, e_tr, b * 8 + 4 + 2 * k + 1, e_trout)
                for k in range(2):
                    act_e.wait_ge(hid_mm, b * 2 + k + 1)
                    nc.scalar.activation(
                        act_exp[:, 4 * k:4 * k + 4, :],
                        slot_ps[:, 1, :].rearrange("p (t e) -> p t e", t=4)[:, :, 0:EI],
                        ACT.Exp, scale=-1.0).then_inc(hid_exp, 1)
                act_e.wait_ge(z_ready, b + 1)
                nc.scalar.activation(router_w[:], pick[0][:], ACT.Exp).then_inc(z_exp, 1)
                for k in range(2):
                    act_e.wait_ge(at_mm, b * 2 + k + 1)
                    nc.scalar.copy(act_t[:, k, :], unit_ps[:, 2, :]).then_inc(at_out, 1)

        @block.gpsimd
        def _(pool):
            nc.gpsimd.memset(v_all[:], 0.0).then_inc(v_zero, 1)
            pool.wait_ge(v_zero, 1)
            nc.gpsimd.memset(v_all[:, :, :, :, HD:HD + 1], 1.0).then_inc(v_ones, 1)
            with pool.Fori(0, B) as b:
                for k in range(2):
                    settled(pool, rot_read, b * TT + 4 * k + 4)
                    nc.gpsimd.tensor_tensor(rot_a, rot_a, rot_b, ALU.add).then_inc(rot_sum, 1)
                    settled(pool, p_mid, b * 2 + k + 1)
                    nc.gpsimd.tensor_tensor(parts_sb[:, k, 2, :, :], rest, parts_sb[:, k, 1, :, :],
                                            ALU.subtract).then_inc(p_lo, 1)

            def values(n, par, wait=True):
                if wait:
                    settled(pool, pv_mm, n * 10 - 10)
                nc.gpsimd.tensor_copy(v_now[:, par, :, :].rearrange("p t d -> p (t d)"),
                                      v_all[:].rearrange("p b g t d -> p (b g) (t d)")[:, n, :]).then_inc(v_here, 1)

            pool.wait_ge(v_ones, 1)
            pool.wait_ge(v_read, B * TT)
            values(0, 0, wait=False)
            values(1, 1, wait=False)
            with pool.Fori(0, 3) as i:
                values(i * 2 + 2, 0)
                values(i * 2 + 3, 1)

            pool.wait_ge(o_normed, NG * 2)
            with pool.Fori(0, B) as b:
                settled(pool, yf_used, b * 8)
                for g in range(KV_HEADS):
                    src = heads_out[:].rearrange("p (b g) t d -> p b g t d", b=B)[:, b, g, :, :]
                    copy = nc.gpsimd.tensor_copy(o_now[:, :, g, :], src)
                copy.then_inc(e_gather, 1)

        @block.vector
        def _(dve):
            dve.wait_ge(cond_e, 1)
            nc.vector.tensor_scalar(cond_exp[:], cond_exp[:], 1.0, None, ALU.add).then_inc(cond_s, 1)
            dve.wait_ge(cond_s, 1)
            nc.vector.reciprocal(cond_exp[:], cond_exp[:]).then_inc(cond_s, 1)
            dve.wait_ge(cond_s, 2)
            nc.vector.tensor_tensor(cond_silu[:], cond_sb[:], cond_exp[:], ALU.mult).then_inc(cond_r, 1)
            dve.wait_ge(cond_r, 2)
            for b in range(B):
                nc.vector.tensor_copy(cond_rep[:, :, b, :], cond_silu[:, :, b:b + 1].to_broadcast([P, DC, P])
                                      ).then_inc(cond_r, 1)
            dve.wait_ge(mod_mm, 2)
            bc = slot_ps[:, 0, :].rearrange("p (j d) -> p j d", j=4)
            nc.vector.tensor_scalar(gate_abs[:], bc, -1.0, 0.25, ALU.mult, ALU.max).then_inc(mod_own, 1)
            dve.wait_ge(mod_own, 2)
            nc.vector.tensor_tensor(gate_abs[:], bc, gate_abs[:], ALU.max).then_inc(mod_own, 1)
            nc.vector.tensor_scalar(gates[:], bc, 0.0, 2.0, ALU.is_ge, ALU.mult).then_inc(mod_own, 1)
            dve.wait_ge(mod_own, 4)
            nc.vector.scalar_tensor_tensor(gates[:], gates[:], -1.0, gate_abs[:], ALU.add, ALU.mult
                                           ).then_inc(mod_ready, 1)
            for j in (2, 6):
                nc.vector.tensor_scalar(mod_cols[:, j:j + 2, :], mod_cols[:, j:j + 2, :], 1.0, None, ALU.add
                                        ).then_inc(mod_own, 1)
            dve.wait_ge(in_w, 16 * 6)
            dve.wait_ge(mod_ready, 1)
            dve.wait_ge(mod_own, 6)
            for b in range(B):
                for c in range(DC):
                    nc.vector.tensor_tensor(wo_gated[:, b, c, :], wo_sb[:, c, :], gates[:, b, :], ALU.mult)
                nc.vector.tensor_tensor(up_gated[:, b, :], up_sb[:], gates[:, 2 + b, :], ALU.mult)
            dve.wait_ge(in_x, 32)

            def spread(ap, shape):
                return ap.to_broadcast(shape)

            def rotate(b, k):
                for t in range(4):
                    tile = 4 * k + t
                    proj = unit_ps[:, t % 2, 0:QK].rearrange("p (h w e) -> p h w e", w=2, e=HD // 2)
                    a4 = rot_a[:, t, :].rearrange("p (h w e) -> p h w e", w=2, e=HD // 2)
                    b4 = rot_b[:, t, :].rearrange("p (h w e) -> p h w e", w=2, e=HD // 2)
                    heads = QK // HD

                    def table(j):
                        return rope_sb[:, tile, j:j + 1, :].to_broadcast([P, heads, HD // 2])

                    dve.wait_ge(qkv_mm, b * TT + tile + 1)
                    for w in range(2):
                        nc.vector.tensor_tensor(a4[:, :, w, :], proj[:, :, w, :], table(0), ALU.mult)
                    nc.vector.tensor_tensor(b4[:, :, 0, :], proj[:, :, 1, :], table(1), ALU.mult)
                    nc.vector.tensor_tensor(b4[:, :, 1, :], proj[:, :, 0, :], table(2), ALU.mult
                                            ).then_inc(rot_read, 1)

            with dve.Fori(0, B) as b:
                settled(dve, h_ready, b * 4)
                nc.vector.tensor_copy(mod_now[:], mod_cols[:, :, b]).then_inc(now_mod, 1)
                for t in range(TT):
                    nc.vector.bn_stats(stats[:, t, :], x_sb[:, b * TT + t, :]).then_inc(ln_own, 1)
                for t in range(TT):
                    settled(dve, ln_own, b * 18 + t + 1)
                    nc.vector.bn_aggr(mean_var[:, t, :], stats[:, t, :]).then_inc(ln_own, 1)
                dve.wait_ge(ln_own, b * 18 + 16)
                nc.vector.tensor_scalar(var_eps[:], mean_var[:, :, 1], EPS, None, ALU.add).then_inc(ln_var, 1)
                dve.wait_ge(ln_std, b + 1)
                nc.vector.reciprocal(rstd[:], std[:]).then_inc(ln_own, 2)
                dve.wait_ge(ln_own, b * 18 + 18)
                dve.wait_ge(x_t, b * 4)
                for t in range(TT):
                    if t == 0:
                        settled(dve, ln_own, b * 18 + 18)
                    nc.vector.tensor_scalar(normed[:, t, :], x_sb[:, b * TT + t, :], mean_var[:, t, 0:1],
                                            rstd[:, t:t + 1], ALU.subtract, ALU.mult).then_inc(ln_x, 1)
                for k in range(2):
                    dve.wait_ge(p_hi, b * 2 + k)
                    dve.wait_ge(p_rest, b * 2 + k)
                    rotate(b, k)
                    dve.wait_ge(p_hi, b * 2 + k + 1)
                    dve.wait_ge(p_lo, b * 2 + k)
                    nc.vector.tensor_tensor(rest, rot_a, parts_sb[:, k, 0, :, :], ALU.subtract).then_inc(p_rest, 1)

            def take_max(n, slot, where):
                tile, head, heads = SLOTS[slot]
                keys = (tile + 1) * P
                dve.wait_ge(slot_mm, n * NSLOTS + slot + 1)
                src = slot_ps[:, where % 2, :].rearrange("p (j k) -> p j k", j=heads)[:, :, 0:keys]
                nc.vector.tensor_reduce(neg_max[:, tile, head:head + heads], src, AX.X, ALU.max, negate=True
                                        ).then_inc(slot_max, 1)

            def split_max(n, half, slots_done):
                tiles = slice(4 * half, 4 * half + 4)
                dve.wait_ge(slot_max, slots_done)
                if not (isinstance(n, int) and n == 0):
                    dve.wait_ge(rows_mm, n * 2 + half - 1)
                nc.vector.tensor_copy(max_parts[:, tiles, :, 0], neg_max[:, tiles, :]).then_inc(hi_own, 1)
                dve.wait_ge(hi_own, n * 2 + half + 1)
                nc.vector.tensor_tensor(max_parts[:, tiles, :, 1], neg_max[:, tiles, :],
                                        max_parts[:, tiles, :, 0], ALU.subtract).then_inc(max_split, 1)

            def normalise(n, half):
                bank = out_ps[:].rearrange("p (t h c) -> p t h c", t=4, h=GROUP)
                dve.wait_ge(o_turned, n * 2 + half + 1)
                nc.vector.reciprocal(inv_sum[:], bank[:, :, :, HD]).then_inc(o_inv, 1)
                dve.wait_ge(o_inv, n * 2 + half + 1)
                dst = heads_out[:, n, 4 * half:4 * half + 4, :].rearrange("p t (h c) -> p (t h) c", c=HD)
                nc.vector.tensor_tensor(
                    dst, bank.rearrange("p t h c -> p (t h) c")[:, :, 0:HD],
                    inv_sum[:].rearrange("p t (h a) -> p (t h) a", a=1).to_broadcast([P, 16, HD]),
                    ALU.mult).then_inc(o_normed, 1)

            def attend(n, first=False, last=False):
                for w in range(4):
                    take_max(n, RING[w][1], w)
                split_max(n, 1, n * NSLOTS + NSLOTS)
                if not last:
                    take_max(n + 1, RING[4][1], 4)
                if not first:
                    normalise(n - 1, 1)
                if not last:
                    for w in (5, 7, 8, 9, 10):
                        take_max(n + 1, RING[w][1], w)
                    split_max(n + 1, 0, n * NSLOTS + NSLOTS + 6)
                normalise(n, 0)
                if not last:
                    for w in (11, 12, *range(14, len(RING))):
                        take_max(n + 1, RING[w][1], w)

            for w in (4, 5, 7, 8, 9, 10):
                take_max(0, RING[w][1], w)
            split_max(0, 0, 6)
            for w in (11, 12, *range(14, len(RING))):
                take_max(0, RING[w][1], w)
            attend(0, first=True)
            with dve.Fori(0, 3) as i:
                attend(i * 2 + 1)
                attend(i * 2 + 2)
            attend(7, last=True)
            normalise(7, 1)

            CHAIN = 21
            EXPERT_ROW = [P, TT, EXPERTS]
            with dve.Fori(0, B) as b:
                for t in range(TT):
                    settled(dve, yf_mm, b * 16 + t + 1)
                    nc.vector.tensor_tensor(x1[:, t, :], unit_ps[:, t % 2, 0:D], x_sb[:, b * TT + t, :],
                                            ALU.add).then_inc(yf_used, 1)
                for t in range(TT):
                    dve.wait_ge(yf_used, b * 16 + t + 1)
                    nc.vector.bn_stats(stats[:, t, :], x1[:, t, :]).then_inc(e_own, 1)
                for t in range(TT):
                    settled(dve, e_own, b * 17 + t + 1)
                    nc.vector.bn_aggr(mean_var[:, t, :], stats[:, t, :]).then_inc(e_own, 1)
                dve.wait_ge(e_own, b * 17 + 16)
                nc.vector.tensor_scalar(var_eps[:], mean_var[:, :, 1], EPS, None, ALU.add).then_inc(e_var, 1)
                nc.vector.tensor_copy(mod_now[:], mod_cols[:, :, b])
                dve.wait_ge(e_std, b + 1)
                nc.vector.reciprocal(rstd[:], std[:]).then_inc(e_own, 1)
                for t in range(TT):
                    dve.wait_ge(e_own, b * 17 + 17)
                    nc.vector.tensor_scalar(normed[:, t, :], x1[:, t, :], mean_var[:, t, 0:1],
                                            rstd[:, t:t + 1], ALU.subtract, ALU.mult).then_inc(e_norm, 1)

                chain = [0]

                def link(ins):
                    chain[0] += 1
                    ins.then_inc(e_chain, 1)
                    dve.wait_ge(e_chain, b * CHAIN + chain[0])

                hid = slot_ps[:, 1, :].rearrange("p (t e) -> p t e", t=4)
                for k in range(2):
                    quad = slice(4 * k, 4 * k + 4)
                    dve.wait_ge(hid_exp, b * 2 + k + 1)
                    nc.vector.tensor_copy(logits[:, quad, :], hid[:, :, EI:EI + EXPERTS])
                    link(nc.vector.tensor_scalar(act_exp[:, quad, :], act_exp[:, quad, :], 1.0, None, ALU.add))
                    link(nc.vector.reciprocal(act_exp[:, quad, :], act_exp[:, quad, :]))
                    nc.vector.tensor_tensor(act[:, quad, :], hid[:, :, 0:EI], act_exp[:, quad, :], ALU.mult
                                            ).then_inc(hid_used, 1)
                dve.wait_ge(hid_used, b * 2 + 2)

                def row(j):
                    return row_stat[:, j:j + 1, :].rearrange("p a t -> p t a").to_broadcast(EXPERT_ROW)

                def reduce(j, src, op):
                    link(nc.vector.tensor_reduce(row_stat[:, j, :], src, AX.X, op))

                ranks = rank_sb[:].rearrange("p (a e) -> p a e", a=1).to_broadcast(EXPERT_ROW)
                reduce(0, logits[:], ALU.max)
                nc.vector.tensor_tensor(pick[0][:], logits[:], row(0), ALU.subtract).then_inc(z_ready, 1)
                dve.wait_ge(z_exp, b + 1)
                reduce(1, router_w[:], ALU.add)
                link(nc.vector.reciprocal(row_stat[:, 2, :], row_stat[:, 1, :]))
                link(nc.vector.tensor_tensor(router_w[:], router_w[:], row(2), ALU.mult))
                reduce(3, router_w[:], ALU.max)
                link(nc.vector.tensor_tensor(pick[0][:], router_w[:], row(3), ALU.is_ge))
                link(nc.vector.tensor_tensor(pick[0][:], pick[0][:], ranks, ALU.mult))
                reduce(4, pick[0][:], ALU.max)
                link(nc.vector.tensor_tensor(pick[1][:], pick[0][:], row(4), ALU.is_equal))
                link(nc.vector.scalar_tensor_tensor(pick[2][:], pick[1][:], -2.0, router_w[:], ALU.mult, ALU.add))
                reduce(5, pick[2][:], ALU.max)
                link(nc.vector.tensor_tensor(pick[3][:], pick[2][:], row(5), ALU.is_ge))
                link(nc.vector.tensor_tensor(pick[3][:], pick[3][:], ranks, ALU.mult))
                reduce(0, pick[3][:], ALU.max)
                link(nc.vector.tensor_tensor(pick[4][:], pick[3][:], row(0), ALU.is_equal))
                link(nc.vector.tensor_tensor(pick[1][:], pick[1][:], pick[4][:], ALU.add))
                nc.vector.tensor_tensor(router_w[:], router_w[:], pick[1][:], ALU.mult).then_inc(e_chain, 1)
                chain[0] += 1
                dve.wait_ge(e_chain, b * CHAIN + chain[0])
                assert chain[0] == CHAIN, chain[0]
                for k in range(2):
                    quad = slice(4 * k, 4 * k + 4)
                    gate = router_w[:, quad, :].rearrange("p t (e a) -> p (t e) a", a=1).to_broadcast(
                        [P, 4 * EXPERTS, INNER])
                    own = act[:, quad, :].rearrange("p t (e i) -> p (t e) i", i=INNER)
                    nc.vector.tensor_tensor(own, own, gate, ALU.mult).then_inc(act_gated, 1)
                for t in range(TT):
                    dve.wait_ge(yf_mm, b * 16 + TT + t + 1)
                    if t == 0:
                        dve.wait_ge(y_out, b * 16 * TT)
                    nc.vector.tensor_tensor(y_sb[:, t, :], unit_ps[:, t % 2, 0:D], x1[:, t, :], ALU.add
                                            ).then_inc(yf_used, 1)


def constants():
    bf = mybir.dt.np(BF16)
    half = HD // 2
    theta = (1.0 / np.float32(10000.0) ** (np.arange(half, dtype=np.float32) / np.float32(half))).astype(np.float32)
    freqs = np.outer(np.arange(T, dtype=np.float32), theta).astype(np.float32)
    cos, sin = np.cos(freqs), np.sin(freqs)
    scale = np.float32(HD ** -0.25)
    table = np.stack([cos * scale, -sin * scale, sin * scale], axis=1).astype(np.float32)
    rope = np.ascontiguousarray(table.reshape(TT, P, 3, half).transpose(1, 0, 2, 3))

    slopes = np.power(np.float32(2.0), -8.0 * np.arange(1, HEADS + 1, dtype=np.float32) / HEADS).astype(np.float32)
    parts, left = [], slopes.copy()
    for _ in range(3):
        part = left.astype(bf).astype(np.float32)
        parts.append(part)
        left = left - part
    pos = np.arange(T)
    q_tile, k_tile, k_in = pos // P, pos // P * P, pos % P
    q_const = np.zeros((HEADS, FEATURE_ROW, T), np.float32)
    k_const = np.zeros((FEATURE_ROW, T), np.float32)
    k_const[0:MAX_PARTS] = 1.0
    r = MAX_PARTS
    for part in parts:
        q_const[:, r] = part[:, None]
        k_const[r] = k_tile
        r += 1
        for bit in (4, 2, 1):
            q_const[:, r] = -part[:, None] * (bit * P) * ((q_tile // bit) % 2)
            k_const[r] = 1.0
            r += 1
    for part in parts:
        q_const[:, r] = part[:, None]
        k_const[r] = k_in
        r += 1
    assert r <= FEATURE_ROW
    q_const = q_const.reshape(KV_HEADS, GROUP, FEATURE_ROW, T).transpose(0, 2, 1, 3)
    q_const = np.ascontiguousarray(np.concatenate([q_const] * B)).astype(bf)
    causal = np.where(np.arange(P)[None, :] > np.arange(P)[:, None], np.float32(MASKED), np.float32(0))
    causal = np.stack([causal, causal.T]).astype(bf)
    rank = np.ascontiguousarray(np.broadcast_to(np.arange(EXPERTS, 0, -1, dtype=np.float32), (P, EXPERTS)))
    return {"rope": rope, "q_const": q_const, "k_const": k_const.astype(bf), "causal": causal,
            "ident": np.eye(P, dtype=np.float32), "rank": rank}


def kernel(**inputs):
    import concourse.bacc as bacc
    from concourse.bass_utils import run_bass_kernel_spmd

    a = {k: np.asarray(v) for k, v in inputs.items()}
    down = a["L0_ffn_down_w"].transpose(2, 0, 1).reshape(D, EI)
    arrays = {
        "x": a["L0_attn_x"],
        "w_qkv": np.concatenate([a["L0_attn_Wq"], a["L0_attn_Wk"], a["L0_attn_Wv"]], axis=1),
        "w_out": a["L0_attn_Wo"],
        "w_hidden_router": np.concatenate([down, a["L0_ffn_router_w"].T], axis=1),
        "w_up": a["L0_ffn_up_w"].transpose(0, 2, 1).reshape(EI, D),
        "cond_t": a["L0_c"].T,
        "w_mod": a["L0_wmod"],
        **constants(),
    }
    arrays = {k: np.ascontiguousarray(v) for k, v in arrays.items()}
    nc = bacc.Bacc("TRN2", target_bir_lowering=False, num_devices=1)
    args = [nc.dram_tensor(f"in_{k}", v.shape, mybir.dt.from_np(v.dtype), kind="ExternalInput").ap()
            for k, v in arrays.items()]
    out = nc.dram_tensor("out_y", (B, T, D), F32, kind="ExternalOutput").ap()
    adaln_block(nc, *args, out)
    r = run_bass_kernel_spmd(nc, [{f"in_{k}": v for k, v in arrays.items()}], core_ids=[0])
    return r.results[0]["out_y"]
```

```python
from contextlib import ExitStack

import numpy as np

import concourse.bass as bass
from concourse import mybir

F32 = mybir.dt.float32
BF16 = mybir.dt.bfloat16
ALU = mybir.AluOpType
ACT = mybir.ActivationFunctionType
AX = mybir.AxisListType

P = 128
B, T, D = 2, 1024, 256
HEADS, KV_HEADS, HD = 16, 4, 16
GROUP = HEADS // KV_HEADS
NG = B * KV_HEADS
TT = T // P
DC = D // P
QC = HEADS * HD
QK = QC + KV_HEADS * HD
QKV = QK + KV_HEADS * HD
HALF = T // 2
EXPERTS, INNER = 8, 16
EI = EXPERTS * INNER
EPS = 1e-5

FEATURE_ROW = 32
MAX_PARTS = 2
Q_PARTS = (0, 0, 1, 1, 0, 2)
K_PARTS = (0, 1, 0, 1, 2, 0)
MASKED = -1e30
KEY_ROW = P - KV_HEADS * HD

UNITS = 36
P_RING = 18
STEPS = []
_u = 0
for _half in range(2):
    for _kt in range(4 * _half):
        STEPS.append((_half, _u, 4, [(_kt, 0, HALF)], 1))
        _u += 4
    STEPS.append((_half, _u, 4, [(4 * _half, 0, 512)], 1))
    STEPS.append((_half, _u + 4, 4, [(4 * _half + 1, 0, 384), (4 * _half + 3, 384, 128)], 1))
    STEPS.append((_half, _u + 8, 2, [(4 * _half + 2, 0, 256)], 2))
    _u += 10
assert _u == UNITS and P_RING * 2 == UNITS and len(STEPS) == 10
FIRST_STEP = (0, 3)
LAST_STEP = (2, 9)
DIAGONAL = (0, 1, 2, 7, 8, 9)

SLOTS = []
for _t in range(TT):
    _per = {0: 4, 1: 4, 2: 2, 3: 2}.get(_t, 1)
    SLOTS += [(_t, _h, _per) for _h in range(0, GROUP, _per)]
NSLOTS = len(SLOTS)
SLOTS_LOW = sum(tile < TT // 2 for tile, _, _ in SLOTS)

RING = ([("max", s) for s in range(8)] + [("rows", 0)] + [("max", s) for s in range(8, NSLOTS)] + [("rows", 1)])
ROWS = (8, 23)
assert len(RING) == NSLOTS + 2 and len(RING) % 2 == 0 and RING[ROWS[0]][0] == RING[ROWS[1]][0] == "rows"

STEADY = ((0,), (1, 2), (3,), (4, 5), (6, 7), (8, 9, 10, 11), (12, 13, 14), (15, 16, 17), (18, 19), (20, 21, 22))
OPENING = tuple(range(9))
FIRST_OWN = ((9, 10, 11, 12), (13, 14, 15, 16), (17, 18, 19, 20, 21, 22))
FIRST_NEXT = ((), (), (), (0, 1, 2, 3), (4, 5, 6, 7), (8, 9, 10, 11), (12, 13, 14), (15, 16, 17), (18, 19), (20, 21, 22))

NBUF = 3
QUADS = B * TT // 4
assert (NG - 2) % NBUF == 0


class Group:

    def __init__(self, loop, const):
        self.loop, self.const = loop, const
        self.index = const if loop is None else loop * NBUF + const
        self.buf = const % NBUF
        self.turn = const // NBUF if loop is None else loop + const // NBUF

    def ahead(self, by):
        return Group(self.loop, self.const + by)


def cycles(eng, attend):
    attend(Group(None, 0), first=True, last=False)
    with eng.Fori(0, (NG - 2) // NBUF) as i:
        for c in range(NBUF):
            attend(Group(i, 1 + c), first=False, last=False)
    attend(Group(None, NG - 1), first=False, last=True)


def adaln_block(nc, x, w_qkv, w_out, w_hidden_router, w_up, cond_t, w_mod, rope, q_const, k_const,
                causal, ident, rank, out):
    ctx = ExitStack()
    with ctx:
        def sb(name, shape, dt=F32):
            return ctx.enter_context(nc.sbuf_tensor(name, shape, dt))

        def sem(name):
            return ctx.enter_context(nc.semaphore(name))

        q_parts = nc.dram_tensor("q_parts", [3, NG * GROUP * HD, T], BF16, kind="Internal").ap()
        k_parts = nc.dram_tensor("k_parts", [3, NG * HD, T], BF16, kind="Internal").ap()

        x_sb = sb("x_sb", [P, B * TT, D])
        wqkv_sb = sb("wqkv_sb", [P, DC, QKV])
        wo_sb = sb("wo_sb", [P, DC, D])
        whr_sb = sb("whr_sb", [P, DC, EI + EXPERTS])
        up_sb = sb("up_sb", [P, D])
        wmod_sb = sb("wmod_sb", [P, DC, 6 * D])
        cond_sb = sb("cond_sb", [P, DC, B])
        cond_exp = sb("cond_exp", [P, DC, B])
        cond_silu = sb("cond_silu", [P, DC, B])
        cond_rep = sb("cond_rep", [P, DC, B, P])
        mod_cols = sb("mod_cols", [P, 8, B])
        mod_now = sb("mod_now", [P, 2, 4])
        gate_abs = sb("gate_abs", [P, 4, D])
        gates = sb("gates", [P, 4, D])
        wo_gated = sb("wo_gated", [P, B, DC, D])
        up_gated = sb("up_gated", [P, B, D])
        rope_sb = sb("rope_sb", [P, TT, 3, HD // 2])
        causal_sb = sb("causal_sb", [P, P], BF16)
        after_sb = sb("after_sb", [P, P], BF16)
        ident_sb = sb("ident_sb", [P, P])
        ident_bf = sb("ident_bf", [P, P], BF16)
        rank_sb = sb("rank_sb", [P, EXPERTS])
        stats = sb("stats", [P, TT, 6])
        mean_var = sb("mean_var", [P, TT, 2])
        mean = sb("mean", [P, B, TT])
        var_eps = sb("var_eps", [P, B, TT])
        std = sb("std", [P, B, TT])
        rstd = sb("rstd", [P, B, TT])
        normed = sb("normed", [P, TT, D])
        h_t = sb("h_t", [P, DC, T])
        v_all = sb("v_all", [P, NG, TT, 32])
        v_now = sb("v_now", [P, NBUF, TT, 32])
        k_stack = [sb(f"k_stack{i}", [P, T], BF16) for i in range(NBUF)]
        q_stack = [sb(f"q_stack{i}", [P, GROUP, T], BF16) for i in range(NBUF)]
        neg_max = sb("neg_max", [P, TT, GROUP])
        max_parts = sb("max_parts", [P, TT, GROUP, MAX_PARTS], BF16)
        max_rows = sb("max_rows", [MAX_PARTS * GROUP, T], BF16)
        o_t = sb("o_t", [P, 512])
        inv_sum = sb("inv_sum", [P, 4, GROUP])
        probs = sb("probs", [P, P_RING, 512])
        rot = probs[:, 0:12, :].rearrange("p (q a) b -> p q (a b)", q=QUADS)[:, :, 0:4 * QK]
        rot_b = probs[:, 12:18, :].rearrange("p (q a) b -> p q (a b)", q=2)[:, :, 0:4 * QK]
        y_sb = probs[:, 0:8, :].rearrange("p a (b c) -> p (a b) c", c=D)
        act_exp = probs[:, 8:10, :].rearrange("p a (b c) -> p (a b) c", c=EI)
        act_now = probs[:, 10:12, :].rearrange("p a (b c) -> p (a b) c", c=EI)
        act_t = probs[:, 12:14, :]
        early = sb("early", [P, QUADS * 3 * 4 * QK], BF16)
        parts_sb = early[:].rearrange("p (q a c) -> p q a c", q=QUADS, a=3)
        late = early[:].bitcast(F32)
        heads_out = late[:, 0:4096].rearrange("p (n t c) -> p n t c", n=NG, t=TT)
        o_now = late[:, 4096:6144].rearrange("p (t g c) -> p t g c", t=TT, g=KV_HEADS)
        early_t = sb("early_t", [P, 2 * 9 * 512], BF16)
        parts_t = early_t[:].rearrange("p (k s t) -> p k s t", k=2, s=9)
        late_t = early_t[:].bitcast(F32)
        o_now_t = late_t[:, 0:2048].rearrange("p (c t) -> p c t", c=DC)
        act = late_t[:, 2048:4096].rearrange("p (t e) -> p t e", e=EI)
        logits = sb("logits", [P, B * TT, EXPERTS])
        router_w = sb("router_w", [P, B * TT, EXPERTS])
        pick = [sb(f"pick{i}", [P, B * TT, EXPERTS]) for i in range(5)]
        row_stat = sb("row_stat", [P, 6, B * TT])

        slot_ps = ctx.enter_context(nc.psum_tensor("slot_ps", [P, 2, 1024], F32))
        unit_ps = ctx.enter_context(nc.psum_tensor("unit_ps", [P, 3, 512], F32))
        out_ps = ctx.enter_context(nc.psum_tensor("out_ps", [P, 512], F32))
        tile_banks = [unit_ps[:, 0, :], unit_ps[:, 1, :], unit_ps[:, 2, :], out_ps[:]]
        fill_banks = [slot_ps[:, 0, 0:512], slot_ps[:, 0, 512:1024], slot_ps[:, 1, 0:512], slot_ps[:, 1, 512:1024],
                      out_ps[:]]

        in_c, in_mod, in_w = sem("in_c"), sem("in_mod"), sem("in_w")
        in_attn, in_late = sem("in_attn"), sem("in_late")
        in_x = [sem(f"in_x{b}") for b in range(B)]
        cond_e, cond_s, cond_r, idents = sem("cond_e"), sem("cond_s"), sem("cond_r"), sem("idents")
        cols_mm, cols_out, cols_one = sem("cols_mm"), sem("cols_out"), sem("cols_one")
        gates_mm, gates_own, gated = sem("gates_mm"), sem("gates_own"), sem("gated")
        v_zero, v_ones = sem("v_zero"), sem("v_ones")
        ln_stat, ln_agg, ln_var, ln_std, ln_inv, ln_x = (sem("ln_stat"), sem("ln_agg"), sem("ln_var"), sem("ln_std"),
                                                         sem("ln_inv"), sem("ln_x"))
        now_mod, x_turned, h_ready = sem("now_mod"), sem("x_turned"), sem("h_ready")
        qkv_mm, rot_read, v_read, rot_sum = sem("qkv_mm"), sem("rot_read"), sem("v_read"), sem("rot_sum")
        p_hi, p_rest, p_mid, p_lo = sem("p_hi"), sem("p_rest"), sem("p_mid"), sem("p_lo")
        fills_mm, q_out, k_out = sem("fills_mm"), sem("q_out"), sem("k_out")
        parts_dma = [sem(f"parts_dma{k}") for k in range(2)]
        loaded = [sem(f"loaded{i}") for i in range(NBUF)]
        slot_mm, slot_max = sem("slot_mm"), sem("slot_max")
        hi_own, max_split, rows_mm, rows_out, rows_in = (sem("hi_own"), sem("max_split"), sem("rows_mm"),
                                                         sem("rows_out"), sem("rows_in"))
        unit_mm, unit_exp, v_here = sem("unit_mm"), sem("unit_exp"), sem("v_here")
        pv_mm, o_copied, o_turned, o_inv, o_normed = (sem("pv_mm"), sem("o_copied"), sem("o_turned"),
                                                      sem("o_inv"), sem("o_normed"))
        o_here, heads_mm, heads_t = sem("o_here"), sem("heads_mm"), sem("heads_t")
        tile_mm, tile_read = sem("tile_mm"), sem("tile_read")
        e_stat, e_agg, e_var, e_std, e_inv, e_x = (sem("e_stat"), sem("e_agg"), sem("e_var"), sem("e_std"),
                                                   sem("e_inv"), sem("e_x"))
        e_now, e_turned, e_h = sem("e_now"), sem("e_turned"), sem("e_h")
        hid_mm, hid_exp, hid_own, hid_read = sem("hid_mm"), sem("hid_exp"), sem("hid_own"), sem("hid_read")
        chain_own, z_ready, z_exp, act_gated = sem("chain_own"), sem("z_ready"), sem("z_exp"), sem("act_gated")
        act_mm, act_out, y_out = sem("act_mm"), sem("act_out"), sem("y_out")
        passed = sem("passed")

        block = ctx.enter_context(nc.Block())

        def settled(eng, semaphore, value):
            eng.wait_ge(semaphore, value)
            eng.sem_inc(passed, 1)

        FREE_TURNS = 2 * DC
        FREE_TILES = 4
        FREE_QUADS = 2
        FREE_Q, FREE_K = 3, 2

        FREE_PARTS = 1

        PARTS_DMA = 16 * 4
        LOADED = 16 * (2 * len(Q_PARTS) + 1)
        ROWS_IN = 16 * GROUP

        @block.sync
        def _(sp):
            for k in range(2):
                sp.sem_inc(parts_dma[k], FREE_PARTS)
            sp.dma_start(cond_sb[:], cond_t.rearrange("(k p) b -> p k b", p=P)).then_inc(in_c, 16)
            sp.dma_start(ident_sb[:], ident).then_inc(in_c, 16)
            sp.dma_start(x_sb[:, 0:TT, :], x[0].rearrange("(t p) d -> p t d", p=P)).then_inc(in_x[0], 16)
            mod_rows = w_mod.rearrange("(k p) n -> p k n", p=P)
            sp.dma_start(wmod_sb[:, :, 0:2 * D], mod_rows[:, :, 0:2 * D]).then_inc(in_mod, 16)
            sp.dma_start(wqkv_sb[:], w_qkv.rearrange("(k p) n -> p k n", p=P)).then_inc(in_w, 16)
            sp.dma_start(rope_sb[:], rope).then_inc(in_w, 16)
            sp.dma_start(x_sb[:, TT:2 * TT, :], x[1].rearrange("(t p) d -> p t d", p=P)).then_inc(in_x[1], 16)
            sp.dma_start(causal_sb[:], causal[0]).then_inc(in_attn, 16)
            sp.dma_start(after_sb[:], causal[1]).then_inc(in_attn, 16)
            for buf in range(NBUF):
                sp.dma_start(k_stack[buf][0:FEATURE_ROW, :], k_const).then_inc(in_attn, 16)
            sp.dma_start(wmod_sb[:, :, 2 * D:6 * D], mod_rows[:, :, 2 * D:6 * D]).then_inc(in_late, 16)
            sp.dma_start(rank_sb[:], rank).then_inc(in_late, 16)
            sp.dma_start(wo_sb[:], w_out.rearrange("(k p) n -> p k n", p=P)).then_inc(in_late, 16)
            sp.dma_start(up_sb[:], w_up).then_inc(in_late, 16)
            sp.dma_start(whr_sb[:], w_hidden_router.rearrange("(k p) n -> p k n", p=P)).then_inc(in_late, 16)

            with sp.Fori(0, B) as b:
                for k in range(2):
                    cols = slice(k * 512, (k + 1) * 512)
                    for part in range(3):
                        sp.wait_ge(q_out, FREE_Q + (b * 2 + k) * 3 + part + 1)
                        dst = q_parts[part, bass.ds(b * D, D), cols].rearrange("(c p) t -> p c t", p=P)
                        sp.dma_start(dst, parts_t[:, k, 2 * part:2 * part + 2, :]).then_inc(parts_dma[k], 16)
                    sp.wait_ge(k_out, FREE_K + (b * 2 + k) * 2 + 2)
                    dst = k_parts[:, bass.ds(b * (P - KEY_ROW), P - KEY_ROW), cols].rearrange("a p t -> p a t")
                    sp.dma_start(dst, parts_t[KEY_ROW:P, k, 6:9, :]).then_inc(parts_dma[k], 16)

            def load(group):
                rows, done, n = GROUP * HD, loaded[group.buf], group.index
                qs, ks = q_stack[group.buf], k_stack[group.buf]
                sp.dma_start(qs[0:FEATURE_ROW, :, :], q_const[n, :, :, :]).then_inc(done, 16)
                for j in range(len(Q_PARTS)):
                    at = slice(FEATURE_ROW + HD * j, FEATURE_ROW + HD * (j + 1))
                    src = q_parts[Q_PARTS[j], bass.ds(n * rows, rows), :].rearrange("(h d) t -> d h t", d=HD)
                    sp.dma_start(qs[at, :, :], src).then_inc(done, 16)
                    sp.dma_start(ks[at, :], k_parts[K_PARTS[j], bass.ds(n * HD, HD), :]).then_inc(done, 16)

            for k in range(2):
                sp.wait_ge(parts_dma[k], FREE_PARTS + PARTS_DMA * B)
            load(Group(None, 0))
            load(Group(None, 1))

            def move_rows(group, half):
                cols = slice(half * HALF, (half + 1) * HALF)
                sp.wait_ge(rows_out, group.index * 2 + half + 1)
                for head in range(GROUP):
                    sp.dma_start(q_stack[group.buf][0:MAX_PARTS, head, cols],
                                 max_rows[MAX_PARTS * head:MAX_PARTS * (head + 1), cols]).then_inc(rows_in, 16)

            move_rows(Group(None, 0), 0)
            for n in range(NG):
                group = Group(None, n)
                move_rows(group, 1)
                if n + 2 < NG:
                    if n > 0:
                        sp.wait_ge(unit_mm, n * UNITS)
                    load(group.ahead(2))
                if n + 1 < NG:
                    move_rows(group.ahead(1), 0)

            with sp.Fori(0, B) as b:
                for k in range(2):
                    sp.wait_ge(tile_read, FREE_TILES + (B * TT) + b * TT + 4 * k + 4)
                    dst = out[bass.ds(b, 1), k * 512:(k + 1) * 512, :].rearrange("a (t p) d -> p (a t) d", p=P)
                    sp.dma_start(dst, y_sb[:, bass.ds(b * TT + 4 * k, 4), :]).then_inc(y_out, 16)
            sp.wait_ge(y_out, 16 * QUADS)

        @block.tensor
        def _(pe):
            pe.sem_inc(x_turned, FREE_TURNS)
            pe.sem_inc(e_turned, FREE_TURNS)
            pe.sem_inc(heads_mm, FREE_QUADS)
            pe.sem_inc(act_mm, FREE_QUADS)

            def columns(blocks, bank):
                for j, first in blocks:
                    for k in range(DC):
                        mm = nc.tensor.matmul(bank[:, 2 * j:2 * j + 2], wmod_sb[:, k, first:first + P],
                                              cond_silu[:, k, :], start=(k == 0), stop=(k == DC - 1))
                mm.then_inc(cols_mm, 1)

            pe.wait_ge(in_mod, 16)
            pe.wait_ge(cond_r, 1)
            columns(((0, 0), (1, P), (2, D), (3, D + P)), out_ps)
            pe.wait_ge(in_w, 16 * 2)
            pe.wait_ge(idents, 1)

            def turn_quad(k, turned):
                for c in range(DC):
                    for t in range(4):
                        mm = nc.tensor.transpose(slot_ps[:, k, c * 512 + t * P:c * 512 + (t + 1) * P],
                                                 normed[:, 4 * k + t, c * P:(c + 1) * P], ident_sb[:])
                    mm.then_inc(turned, 1)

            with pe.Fori(0, B) as b:
                for k in range(2):
                    pe.wait_ge(ln_x, b * TT + 4 * k + 4)
                    pe.wait_ge(h_ready, (b * 2 + k) * DC + DC)
                    turn_quad(k, x_turned)
                for k in range(2):
                    pe.wait_ge(h_ready, FREE_TURNS + (b * 2 + k) * DC + DC)
                    if k == 0:
                        pe.wait_ge(cols_out, 1)
                    for t in range(4):
                        pe.wait_ge(v_read, b * TT + 4 * k + t + 1)
                        for c in range(DC):
                            tok = slice((4 * k + t) * P, (4 * k + t + 1) * P)
                            mm = nc.tensor.matmul(tile_banks[t][:, 0:QKV], h_t[:, c, tok], wqkv_sb[:, c, :],
                                                  start=(c == 0), stop=(c == DC - 1))
                        mm.then_inc(qkv_mm, 1)
            pe.wait_ge(v_read, FREE_TILES + B * TT)
            with pe.Fori(0, QUADS) as q:
                pe.wait_ge(p_lo, q + 1)
                for fill in range(5):
                    if fill < 3:
                        settled(pe, q_out, q * 3 + fill + 1)
                    else:
                        settled(pe, k_out, q * 2 + fill - 2)
                    bank = fill_banks[fill].bitcast(BF16)
                    for s in range(2 if fill < 4 else 1):
                        for t in range(4):
                            col = slice(s * 512 + t * P, s * 512 + (t + 1) * P)
                            part = fill if fill < 3 else 2 * (fill - 3) + s
                            first = t * QK + (s * P if fill < 3 else QK - P)
                            mm = nc.tensor.transpose(bank[:, col], parts_sb[:, q, part, first:first + P], ident_bf[:])
                    mm.then_inc(fills_mm, 1)

            def ring_event(group, where):
                kind, which = RING[where]
                m, buf = group.index, group.buf
                opening = isinstance(m, int) and m == 0
                if where < 2 and not opening:
                    before, of = RING[where - 2], group.ahead(-1).index
                elif where >= 2:
                    before, of = RING[where - 2], m
                else:
                    before = None
                if before is None:
                    pe.wait_ge(q_out, FREE_Q + 3 * QUADS)
                    pe.wait_ge(k_out, FREE_K + 2 * QUADS)
                elif before[0] == "max":
                    pe.wait_ge(slot_max, of * NSLOTS + before[1] + 1)
                else:
                    pe.wait_ge(rows_out, of * 2 + before[1] + 1)
                ps = slot_ps[:, where % 2, :]
                if kind == "rows":
                    pe.wait_ge(max_split, m * 2 + which + 1)
                    bank = ps[:, 0:512].bitcast(BF16)
                    for t in range(4):
                        mm = nc.tensor.transpose(
                            bank[0:MAX_PARTS * GROUP, t * P:(t + 1) * P],
                            max_parts[:, 4 * which + t, :, :].rearrange("p h a -> p (h a)"), ident_bf[:])
                    mm.then_inc(rows_mm, 1)
                    return
                tile, head, heads = SLOTS[which]
                if which == 0:
                    pe.wait_ge(loaded[buf], group.turn * LOADED + LOADED)
                keys = (tile + 1) * P
                stride = 1024 // heads
                for j in range(heads):
                    lhs = q_stack[buf][:, head + j, tile * P:(tile + 1) * P]
                    base = j * stride
                    for lo in range(0, keys, 512):
                        hi = min(keys, lo + 512)
                        opens = (base + lo) % 512 == 0
                        mm = nc.tensor.matmul(ps[:, base + lo:base + hi], lhs, k_stack[buf][:, lo:hi],
                                              start=opens, stop=False, skip_group_check=True)
                for j in range(heads):
                    end = j * stride + keys
                    mm = nc.tensor.matmul(ps[:, end - P:end], ident_bf[:], causal_sb[:], start=False, stop=True,
                                          skip_group_check=True)
                mm.then_inc(slot_mm, 1)

            def scores(group, step, events=()):
                half, first, units, blocks, per = STEPS[step]
                n, buf = group.index, group.buf
                if step in FIRST_STEP:
                    pe.wait_ge(rows_in, (n * 2 + half) * ROWS_IN + ROWS_IN)
                events = list(events)
                for j in range(units):
                    u = first + j
                    if u >= 3 or not (isinstance(n, int) and n == 0):
                        pe.wait_ge(unit_exp, n * UNITS + u - 2)
                    ps = unit_ps[:, u % 3, :]
                    for q in range(per):
                        head = j * per + q
                        for kt, col, width in blocks:
                            at = col + q * width
                            q_lo = max(half * HALF, kt * P)
                            mm = nc.tensor.matmul(ps[:, at:at + width], k_stack[buf][:, kt * P:(kt + 1) * P],
                                                  q_stack[buf][:, head, q_lo:q_lo + width],
                                                  start=(at == 0), stop=(step not in DIAGONAL),
                                                  skip_group_check=True)
                            if step in DIAGONAL:
                                mm = nc.tensor.matmul(ps[:, at:at + P], ident_bf[:], after_sb[:], start=False,
                                                      stop=True, skip_group_check=True)
                    mm.then_inc(unit_mm, 1)
                    for _ in range(-(-len(events) // (units - j))):
                        ring_event(*events.pop(0))

            def weigh(group, step):
                half, first, units, blocks, per = STEPS[step]
                n = group.index
                if step == 0:
                    pe.wait_ge(v_here, n + 1)
                if step in FIRST_STEP and not (isinstance(n, int) and n == 0 and step == 0):
                    pe.wait_ge(o_normed, n * 2 + half)
                pe.wait_ge(unit_exp, n * UNITS + first + units)
                for kt, col, width in blocks:
                    q_lo = max(half * HALF, kt * P) - half * HALF
                    for head in range(GROUP):
                        ring = (first + head // per) % P_RING
                        at = col + (head % per) * width
                        mm = nc.tensor.matmul(out_ps[32 * head:32 * head + 32, q_lo:q_lo + width],
                                              v_now[:, group.buf, kt, :], probs[:, ring, at:at + width],
                                              start=(step in FIRST_STEP), stop=(step in LAST_STEP),
                                              skip_group_check=True)
                mm.then_inc(pv_mm, 1)

            def turn_out(group, half):
                pe.wait_ge(o_copied, group.index * 2 + half + 1)
                for t in range(4):
                    mm = nc.tensor.transpose(out_ps[:, t * P:(t + 1) * P], o_t[:, t * P:(t + 1) * P], ident_sb[:])
                mm.then_inc(o_turned, 1)

            def modulation_rest():
                pe.wait_ge(in_late, 16 * 5)
                columns(((4, 3 * D), (5, 3 * D + P), (6, 4 * D), (7, 4 * D + P)), slot_ps[:, 0, :])
                pe.wait_ge(cond_r, 1 + B)
                pe.wait_ge(rows_out, NG * 2)
                for j, (first, b) in enumerate(((2 * D, 0), (2 * D, 1), (5 * D, 0), (5 * D, 1))):
                    for k in range(DC):
                        mm = nc.tensor.matmul(slot_ps[:, 1, j * D:(j + 1) * D], cond_rep[:, k, b, :],
                                              wmod_sb[:, k, first:first + D], start=(k == 0), stop=(k == DC - 1))
                mm.then_inc(gates_mm, 1)

            def attend(group, first, last):
                before = group.ahead(-1)
                ahead = group.ahead(1)
                own, more = (FIRST_OWN, FIRST_NEXT) if first else ((), STEADY)

                def events(step):
                    out = [(group, w) for w in (own[step] if step < len(own) else ())]
                    return out + ([] if last else [(ahead, w) for w in more[step]])

                if first:
                    for step in range(3):
                        scores(group, step, events(step))
                    weigh(group, 0)
                    weigh(group, 1)
                    ring_event(group, ROWS[1])
                else:
                    scores(group, 0)
                    weigh(before, 9)
                    ring_event(group, ROWS[1])
                    for e in events(0):
                        ring_event(*e)
                    scores(group, 1, events(1))
                    turn_out(before, 1)
                    scores(group, 2, events(2))
                    weigh(group, 0)
                    weigh(group, 1)
                weigh(group, 2)
                scores(group, 3, events(3))
                turn_out(group, 0)
                if last:
                    modulation_rest()
                for step in range(4, 10):
                    scores(group, step, events(step))
                    weigh(group, step - 1)

            pe.wait_ge(in_attn, 16 * (2 + NBUF))
            for w in OPENING:
                ring_event(Group(None, 0), w)
            cycles(pe, attend)
            weigh(Group(None, NG - 1), 9)
            turn_out(Group(None, NG - 1), 1)

            pe.wait_ge(o_normed, 2 * NG)
            pe.wait_ge(gated, 2 * B)
            with pe.Fori(0, B) as b:
                for k in range(2):
                    pe.wait_ge(o_here, b * 2 + k + 1)
                    pe.wait_ge(heads_t, (b * 2 + k) * DC + DC)
                    for c in range(DC):
                        for t in range(4):
                            mm = nc.tensor.transpose(
                                slot_ps[:, k, c * 512 + t * P:c * 512 + (t + 1) * P],
                                o_now[:, 4 * k + t, 2 * c:2 * c + 2, :].rearrange("p g d -> p (g d)"), ident_sb[:])
                    mm.then_inc(heads_mm, 1)
                for k in range(2):
                    pe.wait_ge(heads_t, FREE_TURNS + (b * 2 + k) * DC + DC)
                    for t in range(4):
                        pe.wait_ge(tile_read, b * TT + 4 * k + t + 1)
                        for c in range(DC):
                            mm = nc.tensor.matmul(tile_banks[t][:, 0:D],
                                                  o_now_t[:, c, (4 * k + t) * P:(4 * k + t + 1) * P],
                                                  wo_gated[:, b, c, :], start=(c == 0), stop=(c == DC - 1))
                        mm.then_inc(tile_mm, 1)
            pe.wait_ge(heads_t, FREE_TURNS + QUADS * DC)
            with pe.Fori(0, B) as b:
                for k in range(2):
                    pe.wait_ge(e_x, b * TT + 4 * k + 4)
                    pe.wait_ge(hid_read, b * 2 + k + 1)
                    turn_quad(k, e_turned)
                for k in range(2):
                    pe.wait_ge(e_h, FREE_TURNS + (b * 2 + k) * DC + DC)
                    for t in range(4):
                        for c in range(DC):
                            tok = slice((4 * k + t) * P, (4 * k + t + 1) * P)
                            mm = nc.tensor.matmul(slot_ps[:, k, t * 256:t * 256 + EI + EXPERTS], h_t[:, c, tok],
                                                  whr_sb[:, c, :], start=(c == 0), stop=(c == DC - 1),
                                                  skip_group_check=True)
                    mm.then_inc(hid_mm, 1)
            pe.wait_ge(hid_read, FREE_QUADS + QUADS)
            with pe.Fori(0, B) as b:
                for k in range(2):
                    pe.wait_ge(act_gated, b * 2 + k + 1)
                    pe.wait_ge(act_out, b * 2 + k + 1)
                    for t in range(4):
                        mm = nc.tensor.transpose(slot_ps[:, k, t * P:(t + 1) * P], act_now[:, 4 * k + t, :],
                                                 ident_sb[:])
                    mm.then_inc(act_mm, 1)
                for k in range(2):
                    pe.wait_ge(act_out, FREE_QUADS + b * 2 + k + 1)
                    for t in range(4):
                        pe.wait_ge(tile_read, B * TT + b * TT + 4 * k + t + 1)
                        nc.tensor.matmul(tile_banks[t][:, 0:D], act_t[:, k, t * P:(t + 1) * P],
                                         up_gated[:, b, :], start=True, stop=True).then_inc(tile_mm, 1)

        @block.scalar
        def _(act_e):
            act_e.sem_inc(h_ready, FREE_TURNS)
            act_e.sem_inc(heads_t, FREE_TURNS)
            act_e.sem_inc(v_read, FREE_TILES)
            act_e.sem_inc(e_h, FREE_TURNS)
            act_e.sem_inc(q_out, FREE_Q)
            act_e.sem_inc(act_out, FREE_QUADS)
            act_e.wait_ge(in_c, 16 * 2)
            nc.scalar.activation(cond_exp[:], cond_sb[:], ACT.Exp, scale=-1.0).then_inc(cond_e, 1)
            nc.scalar.copy(ident_bf[:], ident_sb[:]).then_inc(idents, 1)
            act_e.wait_ge(cols_mm, 1)
            nc.scalar.copy(mod_cols[:, 0:4, :].rearrange("p a b -> p (a b)"), out_ps[:, 0:8]).then_inc(cols_out, 1)
            act_e.wait_ge(v_ones, 1)

            def modulate(k, which, turned, value, done):
                for c in range(DC):
                    act_e.wait_ge(turned, value + c)
                    nc.scalar.activation(h_t[:, c, k * 512:(k + 1) * 512], slot_ps[:, k, c * 512:(c + 1) * 512],
                                         ACT.Identity, bias=mod_now[:, which, c:c + 1],
                                         scale=mod_now[:, which, 2 + c:3 + c]).then_inc(done, 1)

            with act_e.Fori(0, B) as b:
                settled(act_e, ln_var, b + 1)
                nc.scalar.activation(std[:, b, :], var_eps[:, b, :], ACT.Sqrt).then_inc(ln_std, 1)
                act_e.wait_ge(now_mod, b * 2 + 2)
                for k in range(2):
                    modulate(k, 0, x_turned, FREE_TURNS + (b * 2 + k) * DC + 1, h_ready)
                for k in range(2):
                    for t in range(4):
                        settled(act_e, rot_read, b * TT + 4 * k + t + 1)
                        nc.scalar.copy(v_all[:, bass.ds(b * KV_HEADS, KV_HEADS), 4 * k + t, 0:HD],
                                       tile_banks[t][:, QK:QKV].rearrange("p (g d) -> p g d", g=KV_HEADS)
                                       ).then_inc(v_read, 1)
            with act_e.Fori(0, QUADS) as q:
                settled(act_e, rot_sum, FREE_QUADS + q + 1)
                nc.scalar.copy(parts_sb[:, q, 0, :], rot[:, q, :]).then_inc(p_hi, 1)
            with act_e.Fori(0, QUADS) as q:
                settled(act_e, p_rest, q + 1)
                nc.scalar.copy(parts_sb[:, q, 1, :], rot[:, q, :]).then_inc(p_mid, 1)
            with act_e.Fori(0, B) as b:
                for k in range(2):
                    for fill in range(3):
                        if fill == 0:
                            act_e.wait_ge(parts_dma[k], FREE_PARTS + b * PARTS_DMA)
                        act_e.wait_ge(fills_mm, (b * 2 + k) * 5 + fill + 1)
                        bank = fill_banks[fill].bitcast(BF16)
                        nc.scalar.copy(parts_t[:, k, 2 * fill:2 * fill + 2, :],
                                       bank.rearrange("p (s t) -> p s t", s=2)).then_inc(q_out, 1)

            def exps(group, step, lo, hi):
                first, n = STEPS[step][1], group.index
                for u in range(first + lo, first + hi):
                    user = u - P_RING
                    steps_before = sum(s[1] <= user % UNITS for s in STEPS)
                    if user >= 0:
                        act_e.wait_ge(pv_mm, n * 10 + steps_before)
                    elif not (isinstance(n, int) and n == 0):
                        act_e.wait_ge(pv_mm, n * 10 - 10 + steps_before)
                    act_e.wait_ge(unit_mm, n * UNITS + u + 1)
                    nc.scalar.activation(probs[:, u % P_RING, :], unit_ps[:, u % 3, :], ACT.Exp).then_inc(unit_exp, 1)

            def rows_copy(group, half):
                index = group.index * 2 + half
                act_e.wait_ge(rows_mm, index + 1)
                if not (isinstance(index, int) and index < 2):
                    act_e.wait_ge(rows_in, index * ROWS_IN - ROWS_IN)
                nc.scalar.copy(max_rows[:, half * HALF:(half + 1) * HALF],
                               slot_ps[0:MAX_PARTS * GROUP, ROWS[half] % 2, 0:512].bitcast(BF16)[:, 0:512]
                               ).then_inc(rows_out, 1)

            def out_copy(group, half):
                n = group.index
                act_e.wait_ge(pv_mm, n * 10 + LAST_STEP[half] + 1)
                if not (isinstance(n, int) and n == 0 and half == 0):
                    act_e.wait_ge(o_turned, n * 2 + half)
                nc.scalar.copy(o_t[:], out_ps[:]).then_inc(o_copied, 1)

            def attend(group, first, last):
                exps(group, 0, 0, 4)
                if first:
                    exps(group, 1, 0, 4)
                    exps(group, 2, 0, 2)
                    rows_copy(group, 1)
                else:
                    out_copy(group.ahead(-1), 1)
                    rows_copy(group, 1)
                    exps(group, 1, 0, 4)
                    exps(group, 2, 0, 2)
                exps(group, 3, 0, 2)
                out_copy(group, 0)
                exps(group, 3, 2, 4)
                if last:
                    act_e.wait_ge(cols_mm, 2)
                    nc.scalar.copy(mod_cols[:, 4:8, :].rearrange("p a b -> p (a b)"), slot_ps[:, 0, 8:16]
                                   ).then_inc(cols_out, 1)
                exps(group, 4, 0, 4)
                exps(group, 5, 0, 2)
                if not last:
                    rows_copy(group.ahead(1), 0)
                exps(group, 5, 2, 4)
                for step in range(6, 10):
                    exps(group, step, 0, STEPS[step][2])

            rows_copy(Group(None, 0), 0)
            cycles(act_e, attend)
            out_copy(Group(None, NG - 1), 1)

            with act_e.Fori(0, B) as b:
                for k in range(2):
                    act_e.wait_ge(heads_mm, FREE_QUADS + b * 2 + k + 1)
                    for c in range(DC):
                        nc.scalar.copy(o_now_t[:, c, k * 512:(k + 1) * 512],
                                       slot_ps[:, k, c * 512:(c + 1) * 512]).then_inc(heads_t, 1)
            with act_e.Fori(0, B) as b:
                settled(act_e, e_var, b + 1)
                nc.scalar.activation(std[:, b, :], var_eps[:, b, :], ACT.Sqrt).then_inc(e_std, 1)
            with act_e.Fori(0, B) as b:
                act_e.wait_ge(e_now, b * 2 + 2)
                for k in range(2):
                    modulate(k, 1, e_turned, FREE_TURNS + (b * 2 + k) * DC + 1, e_h)
                for k in range(2):
                    act_e.wait_ge(hid_mm, b * 2 + k + 1)
                    nc.scalar.activation(
                        act_exp[:, 4 * k:4 * k + 4, :],
                        slot_ps[:, k, :].rearrange("p (t e) -> p t e", t=4)[:, :, 0:EI],
                        ACT.Exp, scale=-1.0).then_inc(hid_exp, 1)
            act_e.wait_ge(z_ready, 1)
            nc.scalar.activation(router_w[:], pick[0][:], ACT.Exp).then_inc(z_exp, 1)
            with act_e.Fori(0, B) as b:
                for k in range(2):
                    act_e.wait_ge(act_mm, FREE_QUADS + b * 2 + k + 1)
                    nc.scalar.copy(act_t[:, k, :], slot_ps[:, k, 0:512]).then_inc(act_out, 1)

        @block.gpsimd
        def _(pool):
            pool.sem_inc(rot_sum, FREE_QUADS)
            nc.gpsimd.memset(v_all[:], 0.0).then_inc(v_zero, 1)
            pool.wait_ge(v_zero, 1)
            nc.gpsimd.memset(v_all[:, :, :, HD:HD + 1], 1.0).then_inc(v_ones, 1)
            with pool.Fori(0, B) as b:
                for k in range(2):
                    settled(pool, rot_read, b * TT + 4 * k + 4)
                    quad = rot[:, bass.ds(b * 2 + k, 1), :].rearrange("p a c -> p (a c)")
                    nc.gpsimd.tensor_tensor(quad, quad, rot_b[:, k, :], ALU.add).then_inc(rot_sum, 1)
            with pool.Fori(0, QUADS) as q:
                settled(pool, p_mid, q + 1)
                nc.gpsimd.tensor_tensor(parts_sb[:, q, 2, :], rot[:, q, :], parts_sb[:, q, 1, :], ALU.subtract
                                        ).then_inc(p_lo, 1)

            pool.wait_ge(v_ones, 1)
            pool.wait_ge(v_read, FREE_TILES + B * TT)
            for n in range(NG):
                if n >= NBUF:
                    pool.wait_ge(pv_mm, (n - NBUF) * 10 + 10)
                nc.gpsimd.tensor_copy(v_now[:, n % NBUF, :, :], v_all[:, n, :, :]).then_inc(v_here, 1)

            with pool.Fori(0, B) as b:
                settled(pool, o_normed, b * 2 * KV_HEADS + 2 * KV_HEADS)
                for k in range(2):
                    settled(pool, heads_mm, b * 2 + k + 1)
                    quad = slice(4 * k, 4 * k + 4)
                    nc.gpsimd.tensor_copy(
                        o_now[:, quad, :, :],
                        heads_out[:, bass.ds(b * KV_HEADS, KV_HEADS), quad, :].rearrange("p g t c -> p t g c")
                    ).then_inc(o_here, 1)

        @block.vector
        def _(dve):
            dve.sem_inc(tile_read, FREE_TILES)
            dve.sem_inc(k_out, FREE_K)
            dve.sem_inc(hid_read, FREE_QUADS)
            dve.wait_ge(cond_e, 1)
            nc.vector.tensor_scalar(cond_exp[:], cond_exp[:], 1.0, None, ALU.add).then_inc(cond_s, 1)
            dve.wait_ge(cond_s, 1)
            nc.vector.reciprocal(cond_exp[:], cond_exp[:]).then_inc(cond_s, 1)
            dve.wait_ge(cond_s, 2)
            nc.vector.tensor_tensor(cond_silu[:], cond_sb[:], cond_exp[:], ALU.mult).then_inc(cond_r, 1)
            dve.wait_ge(cond_r, 1)
            for b in range(B):
                nc.vector.tensor_copy(cond_rep[:, :, b, :], cond_silu[:, :, b:b + 1].to_broadcast([P, DC, P])
                                      ).then_inc(cond_r, 1)

            def statistics(t, b, stat):
                nc.vector.bn_stats(stats[:, t, :], x_sb[:, b * TT + t, :]).then_inc(stat, 1)

            def variances(b, stat, agg, var):
                for t in range(TT):
                    settled(dve, stat, b * TT + t + 1)
                    nc.vector.bn_aggr(mean_var[:, t, :], stats[:, t, :]).then_inc(agg, 1)
                settled(dve, agg, b * TT + TT)
                nc.vector.tensor_scalar(var_eps[:, b, :], mean_var[:, :, 1], EPS, None, ALU.add).then_inc(var, 1)
                nc.vector.tensor_copy(mean[:, b, :], mean_var[:, :, 0])

            def normalised(b, k, turned, inv, done):
                for t in range(4 * k, 4 * k + 4):
                    if t == 4 * k:
                        settled(dve, turned, (b * 2 + k) * DC + DC)
                        settled(dve, inv, b + 1)
                    nc.vector.tensor_scalar(normed[:, t, :], x_sb[:, b * TT + t, :], mean[:, b, t:t + 1],
                                            rstd[:, b, t:t + 1], ALU.subtract, ALU.mult).then_inc(done, 1)

            def rotate(b, k, t):
                tile, heads = 4 * k + t, QK // HD
                a = rot[:, bass.ds(b * 2 + k, 1), t * QK:(t + 1) * QK].rearrange("p a (s e) -> p (a s) e", e=HD // 2)
                b4 = rot_b[:, k, t * QK:(t + 1) * QK].rearrange("p (h w e) -> p h w e", w=2, e=HD // 2)
                proj = tile_banks[t][:, 0:QK]
                halves = proj.rearrange("p (h w e) -> p h w e", w=2, e=HD // 2)

                def table(j, count):
                    return rope_sb[:, tile, j:j + 1, :].to_broadcast([P, count, HD // 2])

                settled(dve, qkv_mm, b * TT + tile + 1)
                nc.vector.tensor_tensor(a, proj.rearrange("p (s e) -> p s e", e=HD // 2), table(0, 2 * heads), ALU.mult)
                nc.vector.tensor_tensor(b4[:, :, 0, :], halves[:, :, 1, :], table(1, heads), ALU.mult)
                nc.vector.tensor_tensor(b4[:, :, 1, :], halves[:, :, 0, :], table(2, heads), ALU.mult
                                        ).then_inc(rot_read, 1)

            def shift_and_scale(b, which, ready):
                first = 4 * which
                nc.vector.tensor_copy(mod_now[:, which, 0:2], mod_cols[:, first:first + 2, b]).then_inc(ready, 1)
                nc.vector.tensor_scalar(mod_now[:, which, 2:4], mod_cols[:, first + 2:first + 4, b], 1.0, None, ALU.add
                                        ).then_inc(ready, 1)

            dve.wait_ge(in_x[0], 16)
            with dve.Fori(0, B) as b:
                for t in range(TT):
                    statistics(t, b, ln_stat)
                variances(b, ln_stat, ln_agg, ln_var)
                dve.wait_ge(cols_out, 1)
                settled(dve, h_ready, b * QUADS + QUADS)
                shift_and_scale(b, 0, now_mod)
                settled(dve, ln_std, b + 1)
                nc.vector.reciprocal(rstd[:, b, :], std[:, b, :]).then_inc(ln_inv, 1)
                for k in range(2):
                    normalised(b, k, x_turned, ln_inv, ln_x)
                dve.wait_ge(in_w, 16 * 2)
                for k in range(2):
                    settled(dve, rot_sum, b * 2 + k + 1)
                    for t in range(4):
                        rotate(b, k, t)
                dve.wait_ge(in_x[1], 16)
            with dve.Fori(0, QUADS) as q:
                settled(dve, p_hi, q + 1)
                nc.vector.tensor_tensor(rot[:, q, :], rot[:, q, :], parts_sb[:, q, 0, :], ALU.subtract
                                        ).then_inc(p_rest, 1)
            with dve.Fori(0, B) as b:
                for k in range(2):
                    dve.wait_ge(parts_dma[k], FREE_PARTS + b * PARTS_DMA)
                    for fill, sets in ((3, 2), (4, 1)):
                        dve.wait_ge(fills_mm, (b * 2 + k) * 5 + fill + 1)
                        bank = fill_banks[fill].bitcast(BF16)[KEY_ROW:P, 0:sets * 512]
                        nc.vector.tensor_copy(parts_t[KEY_ROW:P, k, 2 * fill:2 * fill + sets, :],
                                              bank.rearrange("p (s t) -> p s t", s=sets)).then_inc(k_out, 1)

            def take_max(group, where):
                kind, slot = RING[where]
                if kind == "rows":
                    return
                tile, head, heads = SLOTS[slot]
                keys = (tile + 1) * P
                dve.wait_ge(slot_mm, group.index * NSLOTS + slot + 1)
                src = slot_ps[:, where % 2, :].rearrange("p (j k) -> p j k", j=heads)[:, :, 0:keys]
                nc.vector.tensor_reduce(neg_max[:, tile, head:head + heads], src, AX.X, ALU.max, negate=True
                                        ).then_inc(slot_max, 1)

            def split_max(group, half):
                tiles = slice(4 * half, 4 * half + 4)
                n = group.index
                dve.wait_ge(slot_max, n * NSLOTS + (NSLOTS if half else SLOTS_LOW))
                if not (isinstance(n, int) and n == 0):
                    dve.wait_ge(rows_mm, n * 2 + half - 1)
                nc.vector.tensor_copy(max_parts[:, tiles, :, 0], neg_max[:, tiles, :]).then_inc(hi_own, 1)
                dve.wait_ge(hi_own, n * 2 + half + 1)
                nc.vector.tensor_tensor(max_parts[:, tiles, :, 1], neg_max[:, tiles, :],
                                        max_parts[:, tiles, :, 0], ALU.subtract).then_inc(max_split, 1)

            def normalise(group, half):
                n = group.index
                bank = out_ps[:].rearrange("p (t h c) -> p t h c", t=4, h=GROUP)
                dve.wait_ge(o_turned, n * 2 + half + 1)
                nc.vector.reciprocal(inv_sum[:], bank[:, :, :, HD]).then_inc(o_inv, 1)
                dve.wait_ge(o_inv, n * 2 + half + 1)
                dst = heads_out[:, n, 4 * half:4 * half + 4, :].rearrange("p t (h c) -> p (t h) c", c=HD)
                nc.vector.tensor_tensor(
                    dst, bank.rearrange("p t h c -> p (t h) c")[:, :, 0:HD],
                    inv_sum[:].rearrange("p t (h a) -> p (t h) a", a=1).to_broadcast([P, 16, HD]),
                    ALU.mult).then_inc(o_normed, 1)

            def gate_weights():
                dve.wait_ge(gates_mm, 1)
                both = slot_ps[:, 1, :].rearrange("p (j d) -> p j d", j=4)
                nc.vector.tensor_scalar(gate_abs[:], both, -1.0, 0.25, ALU.mult, ALU.max).then_inc(gates_own, 1)
                nc.vector.tensor_scalar(gates[:], both, 0.0, 2.0, ALU.is_ge, ALU.mult).then_inc(gates_own, 1)
                dve.wait_ge(gates_own, 2)
                nc.vector.tensor_tensor(gate_abs[:], both, gate_abs[:], ALU.max).then_inc(gates_own, 1)
                dve.wait_ge(gates_own, 3)
                nc.vector.scalar_tensor_tensor(gates[:], gates[:], -1.0, gate_abs[:], ALU.add, ALU.mult
                                               ).then_inc(gates_own, 1)
                dve.wait_ge(in_late, 16 * 5)
                dve.wait_ge(gates_own, 4)
                for b in range(B):
                    gate = gates[:, b:b + 1, :].to_broadcast([P, DC, D])
                    nc.vector.tensor_tensor(wo_gated[:, b, :, :], wo_sb[:], gate, ALU.mult).then_inc(gated, 1)
                    nc.vector.tensor_tensor(up_gated[:, b, :], up_sb[:], gates[:, 2 + b, :], ALU.mult
                                            ).then_inc(gated, 1)

            def attend(group, first, last):
                before, ahead = group.ahead(-1), group.ahead(1)
                if first:
                    for step in FIRST_OWN:
                        for w in step:
                            take_max(group, w)
                    split_max(group, 1)
                    for w in range(4):
                        take_max(ahead, w)
                    normalise(group, 0)
                elif last:
                    normalise(before, 1)
                    normalise(group, 0)
                    gate_weights()
                    return
                else:
                    for w in range(3):
                        take_max(ahead, w)
                    normalise(before, 1)
                    take_max(ahead, 3)
                for w in range(4 if not last else 0, SLOTS_LOW):
                    take_max(ahead, w)
                split_max(ahead, 0)
                if not first:
                    normalise(group, 0)
                for w in range(SLOTS_LOW, len(RING)):
                    take_max(ahead, w)
                split_max(ahead, 1)

            for w in range(SLOTS_LOW):
                take_max(Group(None, 0), w)
            split_max(Group(None, 0), 0)
            for w in OPENING[SLOTS_LOW:]:
                take_max(Group(None, 0), w)
            cycles(dve, attend)
            normalise(Group(None, NG - 1), 1)

            with dve.Fori(0, B) as b:
                for t in range(TT):
                    settled(dve, tile_mm, b * TT + t + 1)
                    here = x_sb[:, bass.ds(b * TT + t, 1), :].rearrange("p a d -> p (a d)")
                    nc.vector.tensor_tensor(here, tile_banks[t % 4][:, 0:D], here, ALU.add).then_inc(tile_read, 1)
                for t in range(TT):
                    settled(dve, tile_read, FREE_TILES + b * TT + t + 1)
                    statistics(t, b, e_stat)
                variances(b, e_stat, e_agg, e_var)
            with dve.Fori(0, B) as b:
                dve.wait_ge(cols_out, 2)
                settled(dve, e_h, b * QUADS + QUADS)
                shift_and_scale(b, 1, e_now)
                settled(dve, e_std, b + 1)
                nc.vector.reciprocal(rstd[:, b, :], std[:, b, :]).then_inc(e_inv, 1)
                for k in range(2):
                    normalised(b, k, e_turned, e_inv, e_x)
                for k in range(2):
                    quad = slice(4 * k, 4 * k + 4)
                    here = bass.ds(b * TT + 4 * k, 4)
                    hid = slot_ps[:, k, :].rearrange("p (t e) -> p t e", t=4)
                    settled(dve, hid_exp, b * 2 + k + 1)
                    nc.vector.tensor_copy(logits[:, here, :], hid[:, :, EI:EI + EXPERTS]).then_inc(hid_own, 1)
                    nc.vector.tensor_scalar(act_exp[:, quad, :], act_exp[:, quad, :], 1.0, None, ALU.add
                                            ).then_inc(hid_own, 1)
                    dve.wait_ge(hid_own, (b * 2 + k) * 3 + 2)
                    nc.vector.reciprocal(act_exp[:, quad, :], act_exp[:, quad, :]).then_inc(hid_own, 1)
                    settled(dve, hid_own, (b * 2 + k) * 3 + 3)
                    nc.vector.tensor_tensor(act[:, here, :], hid[:, :, 0:EI], act_exp[:, quad, :], ALU.mult
                                            ).then_inc(hid_read, 1)

            EXPERT_ROW = [P, B * TT, EXPERTS]
            links = [0]

            def link(ins):
                links[0] += 1
                ins.then_inc(chain_own, 1)
                dve.wait_ge(chain_own, links[0])

            def row(j):
                return row_stat[:, j:j + 1, :].rearrange("p a t -> p t a").to_broadcast(EXPERT_ROW)

            def reduce(j, src, op):
                link(nc.vector.tensor_reduce(row_stat[:, j, :], src, AX.X, op))

            ranks = rank_sb[:].rearrange("p (a e) -> p a e", a=1).to_broadcast(EXPERT_ROW)
            dve.wait_ge(hid_own, QUADS * 3)
            reduce(0, logits[:], ALU.max)
            nc.vector.tensor_tensor(pick[0][:], logits[:], row(0), ALU.subtract).then_inc(z_ready, 1)
            dve.wait_ge(z_exp, 1)
            reduce(1, router_w[:], ALU.add)
            link(nc.vector.reciprocal(row_stat[:, 2, :], row_stat[:, 1, :]))
            link(nc.vector.tensor_tensor(router_w[:], router_w[:], row(2), ALU.mult))
            reduce(3, router_w[:], ALU.max)
            link(nc.vector.tensor_tensor(pick[0][:], router_w[:], row(3), ALU.is_ge))
            link(nc.vector.tensor_tensor(pick[0][:], pick[0][:], ranks, ALU.mult))
            reduce(4, pick[0][:], ALU.max)
            link(nc.vector.tensor_tensor(pick[1][:], pick[0][:], row(4), ALU.is_equal))
            link(nc.vector.scalar_tensor_tensor(pick[2][:], pick[1][:], -2.0, router_w[:], ALU.mult, ALU.add))
            reduce(5, pick[2][:], ALU.max)
            link(nc.vector.tensor_tensor(pick[3][:], pick[2][:], row(5), ALU.is_ge))
            link(nc.vector.tensor_tensor(pick[3][:], pick[3][:], ranks, ALU.mult))
            reduce(0, pick[3][:], ALU.max)
            link(nc.vector.tensor_tensor(pick[4][:], pick[3][:], row(0), ALU.is_equal))
            link(nc.vector.tensor_tensor(pick[1][:], pick[1][:], pick[4][:], ALU.add))
            link(nc.vector.tensor_tensor(router_w[:], router_w[:], pick[1][:], ALU.mult))

            dve.wait_ge(hid_read, FREE_QUADS + QUADS)
            with dve.Fori(0, B) as b:
                for k in range(2):
                    settled(dve, act_mm, b * 2 + k + 1)
                    here = bass.ds(b * TT + 4 * k, 4)
                    gate = router_w[:, here, :].rearrange("p t (e a) -> p (t e) a", a=1).to_broadcast(
                        [P, 4 * EXPERTS, INNER])
                    nc.vector.tensor_tensor(
                        act_now[:, 4 * k:4 * k + 4, :].rearrange("p t (e i) -> p (t e) i", i=INNER),
                        act[:, here, :].rearrange("p t (e i) -> p (t e) i", i=INNER), gate, ALU.mult
                    ).then_inc(act_gated, 1)
                for t in range(TT):
                    settled(dve, tile_mm, (B + b) * TT + t + 1)
                    here = bass.ds(b * TT + t, 1)
                    nc.vector.tensor_tensor(y_sb[:, here, :].rearrange("p a d -> p (a d)"),
                                            tile_banks[t % 4][:, 0:D],
                                            x_sb[:, here, :].rearrange("p a d -> p (a d)"), ALU.add
                                            ).then_inc(tile_read, 1)


def constants():
    bf = mybir.dt.np(BF16)
    half = HD // 2
    theta = (1.0 / np.float32(10000.0) ** (np.arange(half, dtype=np.float32) / np.float32(half))).astype(np.float32)
    freqs = np.outer(np.arange(T, dtype=np.float32), theta).astype(np.float32)
    cos, sin = np.cos(freqs), np.sin(freqs)
    scale = np.float32(HD ** -0.25)
    table = np.stack([cos * scale, -sin * scale, sin * scale], axis=1).astype(np.float32)
    rope = np.ascontiguousarray(table.reshape(TT, P, 3, half).transpose(1, 0, 2, 3))

    slopes = np.power(np.float32(2.0), -8.0 * np.arange(1, HEADS + 1, dtype=np.float32) / HEADS).astype(np.float32)
    parts, left = [], slopes.copy()
    for _ in range(3):
        part = left.astype(bf).astype(np.float32)
        parts.append(part)
        left = left - part
    pos = np.arange(T)
    q_tile, k_tile, k_in = pos // P, pos // P * P, pos % P
    q_const = np.zeros((HEADS, FEATURE_ROW, T), np.float32)
    k_const = np.zeros((FEATURE_ROW, T), np.float32)
    k_const[0:MAX_PARTS] = 1.0
    r = MAX_PARTS
    for part in parts:
        q_const[:, r] = part[:, None]
        k_const[r] = k_tile
        r += 1
        for bit in (4, 2, 1):
            q_const[:, r] = -part[:, None] * (bit * P) * ((q_tile // bit) % 2)
            k_const[r] = 1.0
            r += 1
    for part in parts:
        q_const[:, r] = part[:, None]
        k_const[r] = k_in
        r += 1
    assert r <= FEATURE_ROW
    q_const = q_const.reshape(KV_HEADS, GROUP, FEATURE_ROW, T).transpose(0, 2, 1, 3)
    q_const = np.ascontiguousarray(np.concatenate([q_const] * B)).astype(bf)
    causal = np.where(np.arange(P)[None, :] > np.arange(P)[:, None], np.float32(MASKED), np.float32(0))
    causal = np.stack([causal, causal.T]).astype(bf)
    rank = np.ascontiguousarray(np.broadcast_to(np.arange(EXPERTS, 0, -1, dtype=np.float32), (P, EXPERTS)))
    return {"rope": rope, "q_const": q_const, "k_const": k_const.astype(bf), "causal": causal,
            "ident": np.eye(P, dtype=np.float32), "rank": rank}


def kernel(**inputs):
    import concourse.bacc as bacc
    from concourse.bass_utils import run_bass_kernel_spmd

    a = {k: np.asarray(v) for k, v in inputs.items()}
    down = a["L0_ffn_down_w"].transpose(2, 0, 1).reshape(D, EI)
    arrays = {
        "x": a["L0_attn_x"],
        "w_qkv": np.concatenate([a["L0_attn_Wq"], a["L0_attn_Wk"], a["L0_attn_Wv"]], axis=1),
        "w_out": a["L0_attn_Wo"],
        "w_hidden_router": np.concatenate([down, a["L0_ffn_router_w"].T], axis=1),
        "w_up": a["L0_ffn_up_w"].transpose(0, 2, 1).reshape(EI, D),
        "cond_t": a["L0_c"].T,
        "w_mod": a["L0_wmod"],
        **constants(),
    }
    arrays = {k: np.ascontiguousarray(v) for k, v in arrays.items()}
    nc = bacc.Bacc("TRN2", target_bir_lowering=False, num_devices=1)
    args = [nc.dram_tensor(f"in_{k}", v.shape, mybir.dt.from_np(v.dtype), kind="ExternalInput").ap()
            for k, v in arrays.items()]
    out = nc.dram_tensor("out_y", (B, T, D), F32, kind="ExternalOutput").ap()
    adaln_block(nc, *args, out)
    r = run_bass_kernel_spmd(nc, [{f"in_{k}": v for k, v in arrays.items()}], core_ids=[0])
    return r.results[0]["out_y"]
```

```python
from contextlib import ExitStack

import numpy as np

import concourse.bass as bass
from concourse import mybir

F32 = mybir.dt.float32
BF16 = mybir.dt.bfloat16
ALU = mybir.AluOpType
ACT = mybir.ActivationFunctionType
AX = mybir.AxisListType

P = 128
B, T, D = 2, 1024, 256
HEADS, KV_HEADS, HD = 16, 4, 16
GROUP = HEADS // KV_HEADS
NG = B * KV_HEADS
TT = T // P
DC = D // P
QC = HEADS * HD
QK = QC + KV_HEADS * HD
QKV = QK + KV_HEADS * HD
HALF = T // 2
EXPERTS, INNER = 8, 16
EI = EXPERTS * INNER
EPS = 1e-5

FEATURE_ROW = 32
MAX_PARTS = 2
Q_PARTS = (0, 0, 0, 1, 1, 2)
K_PARTS = (0, 1, 2, 0, 1, 0)
MASKED = -1e30
KEY_ROW = P - KV_HEADS * HD

UNITS = 36
P_RING = 18
STEPS = []
_u = 0
for _half in range(2):
    for _kt in range(4 * _half):
        STEPS.append((_half, _u, 4, [(_kt, 0, HALF)], 1))
        _u += 4
    STEPS.append((_half, _u, 4, [(4 * _half, 0, 512)], 1))
    STEPS.append((_half, _u + 4, 4, [(4 * _half + 1, 0, 384), (4 * _half + 3, 384, 128)], 1))
    STEPS.append((_half, _u + 8, 2, [(4 * _half + 2, 0, 256)], 2))
    _u += 10
assert _u == UNITS and P_RING * 2 == UNITS and len(STEPS) == 10
FIRST_STEP = (0, 3)
LAST_STEP = (2, 9)
DIAGONAL = (0, 1, 2, 7, 8, 9)

SLOTS = []
for _t in range(TT):
    _per = {0: 4, 1: 4, 2: 2, 3: 2}.get(_t, 1)
    SLOTS += [(_t, _h, _per) for _h in range(0, GROUP, _per)]
NSLOTS = len(SLOTS)
SLOTS_LOW = sum(tile < TT // 2 for tile, _, _ in SLOTS)

RING = ([("max", s) for s in range(8)] + [("rows", 0)] + [("max", s) for s in range(8, NSLOTS)] + [("rows", 1)])
ROWS = (8, 23)
assert len(RING) == NSLOTS + 2 and len(RING) % 2 == 0 and RING[ROWS[0]][0] == RING[ROWS[1]][0] == "rows"

STEADY = ((), (0, 1, 2, 3), (4,), (5,), (6, 7), (8, 9, 10, 11), (12, 13), (14, 15, 16),
          (17, 18, 19, 20), (21, 22))
LAST_QUAD_AT = 9
OPENING = tuple(range(15))
FIRST_OWN = ((15, 16, 17), (18, 19, 20), (21, 22))
FIRST_WAIT = (0, 1, 2, 3, 4)
FIRST_NEXT = ((), (), (), (5, 6), (7,), (8, 9, 10, 11), (12, 13, 14, 15), (16,), (17, 18, 19),
              (20, 21, 22))
BEFORE_AT = 3
OWN_AT = 6
FIRST_AT = 6
LAST = ((), (("columns", 0, 0),), (("gates", 0, 0), ("gates", 0, 1), ("gates", 0, 2),
         ("gates", 0, 3), ("heads", 0, 0), ("heads", 0, 1)), (("heads", 1, 0),),
        (("heads", 1, 1), ("output", 0, 0), ("output", 0, 1), ("output", 0, 2)),
        (("output", 0, 3),), (("output", 1, 0),), (("output", 1, 1),), (("output", 1, 2),),
        (("output", 1, 3),))
LAST_COPIES = ((), ("columns",), (0,), (), (1,), (), (), (), (), ())

NBUF = 3
LINKS = 17
QUADS = B * TT // 4
assert (NG - 2) % NBUF == 0


class Group:

    def __init__(self, loop, const):
        self.loop, self.const = loop, const
        self.index = const if loop is None else loop * NBUF + const
        self.buf = const % NBUF
        self.turn = const // NBUF if loop is None else loop + const // NBUF

    def ahead(self, by):
        return Group(self.loop, self.const + by)


def cycles(eng, attend):
    attend(Group(None, 0), first=True, last=False)
    with eng.Fori(0, (NG - 2) // NBUF) as i:
        for c in range(NBUF):
            attend(Group(i, 1 + c), first=False, last=False)
    attend(Group(None, NG - 1), first=False, last=True)


def adaln_block(nc, x, w_qkv, w_out, w_hidden_router, w_up, cond_t, w_mod, rope, q_const, k_const,
                causal, ident, rank, out):
    ctx = ExitStack()
    with ctx:
        def sb(name, shape, dt=F32):
            return ctx.enter_context(nc.sbuf_tensor(name, shape, dt))

        def sem(name):
            return ctx.enter_context(nc.semaphore(name))

        q_parts = nc.dram_tensor("q_parts", [3, NG * GROUP * HD, T], BF16, kind="Internal").ap()
        k_parts = nc.dram_tensor("k_parts", [3, NG * HD, T], BF16, kind="Internal").ap()

        x_sb = sb("x_sb", [P, B * TT, D])
        wqkv_sb = sb("wqkv_sb", [P, DC, QKV])
        wo_sb = sb("wo_sb", [P, DC, D])
        whr_sb = sb("whr_sb", [P, DC, EI + EXPERTS])
        up_sb = sb("up_sb", [P, D])
        wmod_sb = sb("wmod_sb", [P, DC, 6 * D])
        cond_sb = sb("cond_sb", [P, DC, B])
        cond_exp = sb("cond_exp", [P, DC, B])
        cond_silu = sb("cond_silu", [P, DC, B])
        cond_rep = sb("cond_rep", [P, DC, B, P])
        mod_cols = sb("mod_cols", [P, 8, B])
        gate_abs = sb("gate_abs", [P, 4, D])
        gates = sb("gates", [P, 4, D])
        wo_gated = sb("wo_gated", [P, B, DC, D])
        up_gated = sb("up_gated", [P, B, D])
        rope_sb = sb("rope_sb", [P, TT, 3, HD // 2])
        causal_sb = sb("causal_sb", [P, P], BF16)
        after_sb = sb("after_sb", [P, P], BF16)
        ident_sb = sb("ident_sb", [P, P])
        ident_bf = sb("ident_bf", [P, P], BF16)
        rank_sb = sb("rank_sb", [P, EXPERTS])
        eps = sb("eps", [P, 1])
        eps_root = sb("eps_root", [P, 1])
        stats = sb("stats", [P, B * TT, 6])
        mean_var = sb("mean_var", [P, B * TT, 2])
        std = sb("std", [P, B * TT])
        rstd = sb("rstd", [P, B * TT])
        normed = sb("normed", [P, TT, D])
        h_t = sb("h_t", [P, DC, T])
        v_all = sb("v_all", [P, NG, TT, 32])
        v_now = sb("v_now", [P, NBUF, TT, 32])
        k_stack = [sb(f"k_stack{i}", [P, T], BF16) for i in range(NBUF)]
        q_stack = [sb(f"q_stack{i}", [P, GROUP, T], BF16) for i in range(NBUF)]
        neg_max = sb("neg_max", [P, TT, GROUP])
        max_parts = sb("max_parts", [P, TT, GROUP, MAX_PARTS], BF16)
        max_rows = sb("max_rows", [MAX_PARTS * GROUP, T], BF16)
        o_t = sb("o_t", [P, 512])
        inv_sum = sb("inv_sum", [P, 4, GROUP])
        probs = sb("probs", [P, P_RING, 512])
        rot = probs[:, 0:12, :].rearrange("p (q a) b -> p q (a b)", q=QUADS)[:, :, 0:4 * QK]
        rot_b = probs[:, 12:18, :].rearrange("p (q a) b -> p q (a b)", q=2)[:, :, 0:4 * QK]
        hid_half = probs[:, 0:4, :].rearrange("p a (b c) -> p (a b) c", c=EI)
        act = probs[:, 4:8, :].rearrange("p a (b c) -> p (a b) c", c=EI)
        act_now = probs[:, 8:12, :].rearrange("p a (b c) -> p (a b) c", c=EI)
        act_t = probs[:, 12:14, :]
        early = sb("early", [P, QUADS * 3 * 4 * QK], BF16)
        parts_sb = early[:].rearrange("p (q a c) -> p q a c", q=QUADS, a=3)
        late = early[:].bitcast(F32)
        heads_out = late[:, 0:4096].rearrange("p (t n c) -> p t n c", n=NG, t=TT)
        early_t = sb("early_t", [P, 2 * 9 * 512], BF16)
        parts_t = early_t[:].rearrange("p (k s t) -> p k s t", k=2, s=9)
        late_t = early_t[:].bitcast(F32)
        o_now_t = late_t[:, 0:2048].rearrange("p (c t) -> p c t", c=DC)
        logits = sb("logits", [P, B * TT, EXPERTS])
        router_w = sb("router_w", [P, B * TT, EXPERTS])
        pick = [sb(f"pick{i}", [P, TT, EXPERTS]) for i in range(5)]
        row_stat = sb("row_stat", [P, 6, TT])

        slot_ps = ctx.enter_context(nc.psum_tensor("slot_ps", [P, 2, 1024], F32))
        unit_ps = ctx.enter_context(nc.psum_tensor("unit_ps", [P, 4, 512], F32))
        out_ps = unit_ps[:, 3, :]
        fill_banks = [[slot_ps[:, 0, 0:512], slot_ps[:, 0, 512:1024], slot_ps[:, 1, 0:512],
                       slot_ps[:, 1, 512:1024], unit_ps[:, 3, :]],
                      [unit_ps[:, 0, :], unit_ps[:, 1, :], unit_ps[:, 2, :], unit_ps[:, 3, :], unit_ps[:, 0, :]]]
        pair_a, pair_b = slot_ps[:, 0, :], slot_ps[:, 1, :]
        pair_c = unit_ps[:, 0:2, :].rearrange("p a b -> p (a b)")
        pair_d = unit_ps[:, 2:4, :].rearrange("p a b -> p (a b)")

        heads_pair = [pair_a, pair_a, pair_b, pair_a]
        output_pair = [pair_b, pair_b, pair_d, pair_c]
        sum_pair = [pair_b, pair_a, pair_b, pair_a]
        hidden_pair = [pair_d, pair_c, pair_b, pair_a]
        experts_pair = [pair_c, pair_d, pair_a, pair_c]
        acts_bank = [pair_d[:, 0:512], pair_d[:, 512:1024], pair_b[:, 0:512], pair_b[:, 512:1024]]

        in_c, in_mod, in_w = sem("in_c"), sem("in_mod"), sem("in_w")
        in_attn, in_late, in_ident = sem("in_attn"), sem("in_late"), sem("in_ident")
        in_x = [sem(f"in_x{q}") for q in range(QUADS)]
        cond_e, cond_s, cond_r, idents = sem("cond_e"), sem("cond_s"), sem("cond_r"), sem("idents")
        cols_mm, cols_out, cols_one = sem("cols_mm"), sem("cols_out"), sem("cols_one")
        gates_mm, gates_own, gated = sem("gates_mm"), sem("gates_own"), sem("gated")
        v_zero, v_ones = sem("v_zero"), sem("v_ones")
        ln_stat, ln_agg, ln_std, ln_inv, ln_x = (sem("ln_stat"), sem("ln_agg"), sem("ln_std"), sem("ln_inv"),
                                                 sem("ln_x"))
        eps_set, x_turned, h_ready = sem("eps_set"), sem("x_turned"), sem("h_ready")
        qkv_mm, rot_read, v_read, rot_sum = sem("qkv_mm"), sem("rot_read"), sem("v_read"), sem("rot_sum")
        p_hi, p_rest, p_mid, p_lo = sem("p_hi"), sem("p_rest"), sem("p_mid"), sem("p_lo")
        q_fill, k_fill, k_out = sem("q_fill"), sem("k_fill"), sem("k_out")
        q_out = [sem(f"q_out{k}") for k in range(2)]
        parts_dma = [sem(f"parts_dma{k}") for k in range(2)]
        loaded_low = sem("loaded_low")
        loaded = [sem(f"loaded{i}") for i in range(NBUF)]
        slot_mm, slot_max = sem("slot_mm"), sem("slot_max")
        hi_own, max_split, rows_mm, rows_out, rows_in = (sem("hi_own"), sem("max_split"), sem("rows_mm"),
                                                         sem("rows_out"), sem("rows_in"))
        unit_mm, unit_exp, v_here = sem("unit_mm"), sem("unit_exp"), sem("v_here")
        pv_mm, o_copied, o_turned, o_inv, o_normed = (sem("pv_mm"), sem("o_copied"), sem("o_turned"),
                                                      sem("o_inv"), sem("o_normed"))
        heads_mm, heads_t, wo_mm, x_sum = sem("heads_mm"), sem("heads_t"), sem("wo_mm"), sem("x_sum")
        e_stat, e_agg, e_std, e_inv, e_x = sem("e_stat"), sem("e_agg"), sem("e_std"), sem("e_inv"), sem("e_x")
        e_turned, e_h = sem("e_turned"), sem("e_h")
        hid_mm, hid_tanh, hid_read = sem("hid_mm"), sem("hid_tanh"), sem("hid_read")
        chain_own, z_ready, z_exp, act_gated = sem("chain_own"), sem("z_ready"), sem("z_exp"), sem("act_gated")
        act_mm, act_out, up_mm, y_sum, y_out = sem("act_mm"), sem("act_out"), sem("up_mm"), sem("y_sum"), sem("y_out")
        passed = sem("passed")

        block = ctx.enter_context(nc.Block())

        def settled(eng, semaphore, value):
            eng.wait_ge(semaphore, value)
            eng.sem_inc(passed, 1)

        def batch_and_cols(q):
            return q // 2, slice(q % 2 * 512, (q % 2 + 1) * 512)

        PARTS_DMA = 16 * 4
        LOADED = 16 * (len(Q_PARTS) + len(K_PARTS) // 3 + 1)
        ROWS_IN = 16 * GROUP

        @block.sync
        def _(sp):
            def tokens(q):
                b, cols = batch_and_cols(q)
                sp.dma_start(x_sb[:, 4 * q:4 * q + 4, :], x[b, cols].rearrange("(t p) d -> p t d", p=P)
                             ).then_inc(in_x[q], 16)

            sp.dma_start(cond_sb[:], cond_t.rearrange("(k p) b -> p k b", p=P)).then_inc(in_c, 16)
            tokens(0)
            mod_rows = w_mod.rearrange("(k p) n -> p k n", p=P)
            sp.dma_start(wmod_sb[:, :, 0:2 * D], mod_rows[:, :, 0:2 * D]).then_inc(in_mod, 16)
            tokens(1)
            sp.dma_start(ident_sb[:], ident).then_inc(in_ident, 16)
            sp.dma_start(wqkv_sb[:], w_qkv.rearrange("(k p) n -> p k n", p=P)).then_inc(in_w, 16)
            tokens(2)
            sp.dma_start(rope_sb[:], rope).then_inc(in_w, 16)
            tokens(3)
            sp.dma_start(causal_sb[:], causal[0]).then_inc(in_attn, 16)
            sp.dma_start(after_sb[:], causal[1]).then_inc(in_attn, 16)
            for buf in range(NBUF):
                sp.dma_start(k_stack[buf][0:FEATURE_ROW, :], k_const).then_inc(in_attn, 16)
            sp.dma_start(wmod_sb[:, :, 2 * D:6 * D], mod_rows[:, :, 2 * D:6 * D]).then_inc(in_late, 16)
            sp.dma_start(rank_sb[:], rank).then_inc(in_late, 16)
            sp.dma_start(wo_sb[:], w_out.rearrange("(k p) n -> p k n", p=P)).then_inc(in_late, 16)
            sp.dma_start(up_sb[:], w_up).then_inc(in_late, 16)
            sp.dma_start(whr_sb[:], w_hidden_router.rearrange("(k p) n -> p k n", p=P)).then_inc(in_late, 16)

            def store_parts(q):
                b, cols = batch_and_cols(q)
                k = q % 2
                for part in range(3):
                    sp.wait_ge(q_out[k], q // 2 * 3 + part + 1)
                    dst = q_parts[part, b * D:(b + 1) * D, cols].rearrange("(c p) t -> p c t", p=P)
                    sp.dma_start(dst, parts_t[:, k, 2 * part:2 * part + 2, :]).then_inc(parts_dma[k], 16)
                sp.wait_ge(k_out, q * 2 + 2)
                dst = k_parts[:, b * (P - KEY_ROW):(b + 1) * (P - KEY_ROW), cols].rearrange("a p t -> p a t")
                sp.dma_start(dst, parts_t[KEY_ROW:P, k, 6:9, :]).then_inc(parts_dma[k], 16)

            def load_constants(group, done):
                sp.dma_start(q_stack[group.buf][0:FEATURE_ROW, :, :], q_const[group.index, :, :, :]).then_inc(done, 16)

            def load(group, done, cols=slice(0, T)):
                rows, n = GROUP * HD, group.index
                qs, ks = q_stack[group.buf], k_stack[group.buf]
                for j in range(len(Q_PARTS)):
                    at = slice(FEATURE_ROW + HD * j, FEATURE_ROW + HD * (j + 1))
                    src = q_parts[Q_PARTS[j], bass.ds(n * rows, rows), cols].rearrange("(h d) t -> d h t", d=HD)
                    sp.dma_start(qs[at, :, cols], src).then_inc(done, 16)
                for j in range(0, len(K_PARTS), 3):
                    at = slice(FEATURE_ROW + HD * j, FEATURE_ROW + HD * (j + 3))
                    sp.dma_start(ks[at, cols], k_parts[:, bass.ds(n * HD, HD), cols]).then_inc(done, 16)

            load_constants(Group(None, 0), loaded_low)
            sp.sem_inc(loaded[0], 16)
            for n in range(1, NBUF):
                load_constants(Group(None, n), loaded[n])
            store_parts(0)
            store_parts(1)
            for k, done in enumerate((loaded_low, loaded[0])):
                sp.wait_ge(parts_dma[k], PARTS_DMA)
                load(Group(None, 0), done, slice(k * HALF, (k + 1) * HALF))
            store_parts(2)

            def move_rows(group, half):
                cols = slice(half * HALF, (half + 1) * HALF)
                sp.wait_ge(rows_out, group.index * 2 + half + 1)
                for head in range(GROUP):
                    sp.dma_start(q_stack[group.buf][0:MAX_PARTS, head, cols],
                                 max_rows[MAX_PARTS * head:MAX_PARTS * (head + 1), cols]).then_inc(rows_in, 16)

            move_rows(Group(None, 0), 0)
            store_parts(3)
            load(Group(None, 1), loaded[1])
            for n in range(NG):
                group = Group(None, n)
                move_rows(group, 1)
                if n + 2 < NG:
                    if n + 2 == KV_HEADS:
                        for k in range(2):
                            sp.wait_ge(parts_dma[k], PARTS_DMA * B)
                    if n > 0:
                        sp.wait_ge(unit_mm, n * UNITS)
                        load_constants(group.ahead(2), loaded[group.ahead(2).buf])
                    load(group.ahead(2), loaded[group.ahead(2).buf])
                if n + 1 < NG:
                    move_rows(group.ahead(1), 0)

            rows = out.rearrange("b (t p) d -> p (b t) d", p=P)
            for half in range(2 * QUADS):
                sp.wait_ge(y_sum, half + 1)
                sp.dma_start(rows[:, 2 * half:2 * half + 2, :], x_sb[:, 2 * half:2 * half + 2, :]).then_inc(y_out, 16)
            sp.wait_ge(y_out, 16 * 2 * QUADS)

        @block.tensor
        def _(pe):
            def columns(blocks, bank):
                for j, first in blocks:
                    for k in range(DC):
                        mm = nc.tensor.matmul(bank[:, 2 * j:2 * j + 2], wmod_sb[:, k, first:first + P],
                                              cond_silu[:, k, :], start=(k == 0), stop=(k == DC - 1))
                mm.then_inc(cols_mm, 1)

            pe.wait_ge(in_mod, 16)
            pe.wait_ge(cond_r, 1)
            columns(((0, 0), (1, P), (2, D), (3, D + P)), out_ps)
            pe.wait_ge(in_ident, 16)

            def turn_quad(q, pair, turned):
                for c in range(DC):
                    for t in range(4):
                        mm = nc.tensor.transpose(pair[:, c * 512 + t * P:c * 512 + (t + 1) * P],
                                                 normed[:, q % 2 * 4 + t, c * P:(c + 1) * P], ident_sb[:])
                    mm.then_inc(turned, 1)

            def turn_input(q):
                pe.wait_ge(ln_x, 4 * q + 4)
                if q >= 2:
                    pe.wait_ge(h_ready, (q - 2) * DC + DC)
                turn_quad(q, slot_ps[:, q % 2, :], x_turned)

            def project(q):
                pe.wait_ge(h_ready, q * DC + DC)
                for t in range(4):
                    if q > 0:
                        pe.wait_ge(v_read, 4 * (q - 1) + t + 1)
                    for c in range(DC):
                        tok = slice((q % 2 * 4 + t) * P, (q % 2 * 4 + t + 1) * P)
                        mm = nc.tensor.matmul(unit_ps[:, t, 0:QKV], h_t[:, c, tok], wqkv_sb[:, c, :],
                                              start=(c == 0), stop=(c == DC - 1))
                    mm.then_inc(qkv_mm, 1)

            def turn_parts(q):
                pe.wait_ge(p_lo, q + 1)
                for fill in range(5):
                    if fill < 3:
                        if q >= 2:
                            pe.wait_ge(q_out[q % 2], (q // 2 - 1) * 3 + fill + 1)
                            pe.wait_ge(k_out, (q - 1) * 2)
                    elif fill == 4 and q % 2 == 1:
                        pe.wait_ge(q_out[1], q // 2 * 3 + 1)
                    elif q > 0:
                        pe.wait_ge(k_out, q * 2)
                    elif fill == 4:
                        pe.wait_ge(v_read, B * TT)
                    bank = fill_banks[q % 2][fill].bitcast(BF16)
                    for s in range(2 if fill < 4 else 1):
                        for t in range(4):
                            col = slice(s * 512 + t * P, s * 512 + (t + 1) * P)
                            part = fill if fill < 3 else 2 * (fill - 3) + s
                            first = t * QK + (s * P if fill < 3 else QK - P)
                            mm = nc.tensor.transpose(bank[:, col], parts_sb[:, q, part, first:first + P], ident_bf[:])
                    mm.then_inc(k_fill if fill >= 3 else q_fill, 1)

            turn_input(0)
            turn_input(1)
            pe.wait_ge(idents, 1)
            pe.wait_ge(cols_out, 1)
            pe.wait_ge(in_w, 16 * 2)
            project(0)
            turn_input(2)
            project(1)
            turn_input(3)
            project(2)
            project(3)
            for q in range(QUADS - 1):
                turn_parts(q)

            def ring_event(group, where):
                kind, which = RING[where]
                m, buf = group.index, group.buf
                opening = isinstance(m, int) and m == 0
                if where < 2 and not opening:
                    before, of = RING[where - 2], group.ahead(-1).index
                elif where >= 2:
                    before, of = RING[where - 2], m
                else:
                    before = None
                if before is None:
                    pe.wait_ge(q_out[0], 3 * 2)
                    pe.wait_ge(k_out, 2 * (QUADS - 1))
                elif before[0] == "max":
                    pe.wait_ge(slot_max, of * NSLOTS + before[1] + 1)
                else:
                    pe.wait_ge(rows_out, of * 2 + before[1] + 1)
                ps = slot_ps[:, where % 2, :]
                if kind == "rows":
                    pe.wait_ge(max_split, m * 2 + which + 1)
                    bank = ps[:, 0:512].bitcast(BF16)
                    for t in range(4):
                        mm = nc.tensor.transpose(
                            bank[0:MAX_PARTS * GROUP, t * P:(t + 1) * P],
                            max_parts[:, 4 * which + t, :, :].rearrange("p h a -> p (h a)"), ident_bf[:])
                    mm.then_inc(rows_mm, 1)
                    return
                tile, head, heads = SLOTS[which]
                if which == 0 and opening:
                    pe.wait_ge(loaded_low, LOADED)
                elif which == (SLOTS_LOW if opening else 0):
                    pe.wait_ge(loaded[buf], group.turn * LOADED + LOADED)
                keys = (tile + 1) * P
                stride = 1024 // heads
                for j in range(heads):
                    lhs = q_stack[buf][:, head + j, tile * P:(tile + 1) * P]
                    base = j * stride
                    for lo in range(0, keys, 512):
                        hi = min(keys, lo + 512)
                        opens = (base + lo) % 512 == 0
                        mm = nc.tensor.matmul(ps[:, base + lo:base + hi], lhs, k_stack[buf][:, lo:hi],
                                              start=opens, stop=False, skip_group_check=True)
                for j in range(heads):
                    end = j * stride + keys
                    mm = nc.tensor.matmul(ps[:, end - P:end], ident_bf[:], causal_sb[:], start=False, stop=True,
                                          skip_group_check=True)
                mm.then_inc(slot_mm, 1)

            def scores(group, step, events=()):
                half, first, units, blocks, per = STEPS[step]
                n, buf = group.index, group.buf
                if step in FIRST_STEP:
                    pe.wait_ge(rows_in, (n * 2 + half) * ROWS_IN + ROWS_IN)
                events = list(events)
                for j in range(units):
                    u = first + j
                    if u >= 3 or not (isinstance(n, int) and n == 0):
                        pe.wait_ge(unit_exp, n * UNITS + u - 2)
                    ps = unit_ps[:, u % 3, :]
                    for q in range(per):
                        head = j * per + q
                        for kt, col, width in blocks:
                            at = col + q * width
                            q_lo = max(half * HALF, kt * P)
                            mm = nc.tensor.matmul(ps[:, at:at + width], k_stack[buf][:, kt * P:(kt + 1) * P],
                                                  q_stack[buf][:, head, q_lo:q_lo + width],
                                                  start=(at == 0), stop=(step not in DIAGONAL),
                                                  skip_group_check=True)
                            if step in DIAGONAL:
                                mm = nc.tensor.matmul(ps[:, at:at + P], ident_bf[:], after_sb[:], start=False,
                                                      stop=True, skip_group_check=True)
                    mm.then_inc(unit_mm, 1)
                    for _ in range(-(-len(events) // (units - j))):
                        event = events.pop(0)
                        if len(event) == 2:
                            ring_event(*event)
                        else:
                            piece_of_output(*event)

            def weigh(group, step):
                half, first, units, blocks, per = STEPS[step]
                n = group.index
                if step == 0:
                    pe.wait_ge(v_here, n + 1)
                if step in FIRST_STEP and not (isinstance(n, int) and n == 0 and step == 0):
                    pe.wait_ge(o_normed, n * 2 + half)
                pe.wait_ge(unit_exp, n * UNITS + first + units)
                for kt, col, width in blocks:
                    q_lo = max(half * HALF, kt * P) - half * HALF
                    for head in range(GROUP):
                        ring = (first + head // per) % P_RING
                        at = col + (head % per) * width
                        mm = nc.tensor.matmul(out_ps[32 * head:32 * head + 32, q_lo:q_lo + width],
                                              v_now[:, group.buf, kt, :], probs[:, ring, at:at + width],
                                              start=(step in FIRST_STEP), stop=(step in LAST_STEP),
                                              skip_group_check=True)
                mm.then_inc(pv_mm, 1)

            def turn_out(group, half):
                pe.wait_ge(o_copied, group.index * 2 + half + 1)
                for t in range(4):
                    mm = nc.tensor.transpose(out_ps[:, t * P:(t + 1) * P], o_t[:, t * P:(t + 1) * P], ident_sb[:])
                mm.then_inc(o_turned, 1)

            def gate_product(j):
                if j == 0:
                    pe.wait_ge(cond_r, 1 + B)
                    pe.wait_ge(rows_out, NG * 2)
                first, b = ((2 * D, 0), (2 * D, 1), (5 * D, 0), (5 * D, 1))[j]
                for k in range(DC):
                    mm = nc.tensor.matmul(slot_ps[:, 1, j * D:(j + 1) * D], cond_rep[:, k, b, :],
                                          wmod_sb[:, k, first:first + D], start=(k == 0), stop=(k == DC - 1))
                mm.then_inc(gates_mm, 1)

            def piece_of_output(kind, q, piece):
                if kind == "columns":
                    pe.wait_ge(in_late, 16 * 5)
                    columns(((4, 3 * D), (5, 3 * D + P), (6, 4 * D), (7, 4 * D + P)), slot_ps[:, 0, :])
                elif kind == "gates":
                    gate_product(piece)
                elif kind == "heads":
                    turn_heads(q, piece)
                else:
                    output(q, piece)

            def attend(group, first, last):
                before = group.ahead(-1)
                ahead = group.ahead(1)
                own, more = (FIRST_OWN, FIRST_NEXT) if first else ((), STEADY)

                def events(step):
                    out = [(group, w) for w in (own[step] if step < len(own) else ())]
                    return out + (list(LAST[step]) if last else [(ahead, w) for w in more[step]])

                if first:
                    for step in range(3):
                        scores(group, step, events(step))
                    weigh(group, 0)
                    weigh(group, 1)
                    ring_event(group, ROWS[1])
                    for w in FIRST_WAIT:
                        ring_event(ahead, w)
                else:
                    scores(group, 0)
                    weigh(before, 9)
                    ring_event(group, ROWS[1])
                    for e in events(0):
                        ring_event(*e)
                    scores(group, 1, events(1))
                    turn_out(before, 1)
                    scores(group, 2, events(2))
                    weigh(group, 0)
                    weigh(group, 1)
                weigh(group, 2)
                scores(group, 3, events(3))
                turn_out(group, 0)
                for step in range(4, 10):
                    scores(group, step, events(step))
                    weigh(group, step - 1)

            def turn_heads(q, c):
                if q == 0:
                    pe.wait_ge(o_normed, 2 * KV_HEADS)
                    pe.wait_ge(cols_out, 2)
                elif q == 1:
                    pe.wait_ge(heads_t, DC)
                elif q == 2:
                    pe.wait_ge(o_normed, 2 * NG)
                    pe.wait_ge(x_sum, 2)
                elif q == 3:
                    pe.wait_ge(heads_t, 2 * DC)
                pair, b = heads_pair[q], q // 2
                for t in range(4):
                    heads = slice(b * KV_HEADS + 2 * c, b * KV_HEADS + 2 * c + 2)
                    mm = nc.tensor.transpose(
                        pair[:, c * 512 + t * P:c * 512 + (t + 1) * P],
                        heads_out[:, q % 2 * 4 + t, heads, :].rearrange("p g d -> p (g d)"), ident_sb[:])
                mm.then_inc(heads_mm, 1)

            def output(q, t):
                pe.wait_ge(heads_t, q * DC + DC)
                pe.wait_ge(gated, q // 2 + 1)
                if q == 0:
                    pe.wait_ge(gates_own, 4)
                elif q == 1:
                    pe.wait_ge(x_sum, 1)
                else:
                    pe.wait_ge(unit_exp, NG * UNITS)
                pair = output_pair[q]
                for c in range(DC):
                    tok = slice((q % 2 * 4 + t) * P, (q % 2 * 4 + t + 1) * P)
                    mm = nc.tensor.matmul(pair[:, t * D:(t + 1) * D], o_now_t[:, c, tok],
                                          wo_gated[:, q // 2, c, :], start=(c == 0), stop=(c == DC - 1),
                                          skip_group_check=True)
                mm.then_inc(wo_mm, 1)

            for w in OPENING:
                if w == LAST_QUAD_AT:
                    turn_parts(QUADS - 1)
                ring_event(Group(None, 0), w)
            pe.wait_ge(q_out[1], 3 * 2)
            pe.wait_ge(k_out, 2 * QUADS)
            cycles(pe, attend)
            weigh(Group(None, NG - 1), 9)
            turn_out(Group(None, NG - 1), 1)


            def turn_sum(q):
                if q < 2:
                    pe.wait_ge(heads_t, (q + 3) * DC)
                else:
                    pe.wait_ge(e_h, (q - 1) * DC)
                pe.wait_ge(e_x, 4 * q + 4)
                turn_quad(q, sum_pair[q], e_turned)

            def hidden(q):
                pe.wait_ge(e_h, q * DC + DC)
                if q < 2:
                    pe.wait_ge(x_sum, q + 3)
                pair = hidden_pair[q]
                for t in range(4):
                    for c in range(DC):
                        tok = slice((q % 2 * 4 + t) * P, (q % 2 * 4 + t + 1) * P)
                        mm = nc.tensor.matmul(pair[:, t * D:t * D + EI + EXPERTS], h_t[:, c, tok], whr_sb[:, c, :],
                                              start=(c == 0), stop=(c == DC - 1), skip_group_check=True)
                mm.then_inc(hid_mm, 1)

            def turn_acts(q):
                pe.wait_ge(act_gated, q + 1)
                pe.wait_ge(hid_read, 1 if q < 2 else 3)
                bank = acts_bank[q]
                for t in range(4):
                    mm = nc.tensor.transpose(bank[:, t * P:(t + 1) * P], act_now[:, 4 * q + t, :], ident_sb[:])
                mm.then_inc(act_mm, 1)

            def experts(q):
                pe.wait_ge(act_out, q + 1)
                if q == 3:
                    pe.wait_ge(y_sum, 2)
                elif q != 1:
                    pe.wait_ge(hid_read, q + 2)
                for t in range(4):
                    mm = nc.tensor.matmul(experts_pair[q][:, t * D:(t + 1) * D],
                                          act_t[:, q % 2, t * P:(t + 1) * P], up_gated[:, q // 2, :],
                                          start=True, stop=True, skip_group_check=True)
                    if t % 2 == 1:
                        mm.then_inc(up_mm, 1)

            def all_pieces(work, q, pieces):
                for piece in range(pieces):
                    work(q, piece)

            all_pieces(turn_heads, 2, DC)
            all_pieces(turn_heads, 3, DC)
            all_pieces(output, 2, 4)
            all_pieces(output, 3, 4)
            for q in (0, 2):
                for work in (turn_sum, hidden):
                    work(q)
                    work(q + 1)
            turn_acts(0)
            turn_acts(1)
            pe.wait_ge(gated, 2 * B)
            experts(0)
            experts(1)
            turn_acts(2)
            turn_acts(3)
            experts(2)
            experts(3)

        @block.scalar
        def _(act_e):
            act_e.wait_ge(in_c, 16)
            nc.scalar.activation(cond_exp[:], cond_sb[:], ACT.Exp, scale=-1.0).then_inc(cond_e, 1)
            act_e.wait_ge(eps_set, 1)
            nc.scalar.activation(eps_root[:], eps[:], ACT.Sqrt)

            def deviations(q, count, agg, done):
                act_e.wait_ge(agg, 4 * (q + count))
                nc.scalar.activation(std[:, 4 * q:4 * (q + count)], mean_var[:, 4 * q:4 * (q + count), 1], ACT.Sqrt,
                                     bias=eps[:]).then_inc(done, 1)

            def modulate(q, first, pair, turned, done):
                b, cols = batch_and_cols(q)
                for c in range(DC):
                    act_e.wait_ge(turned, q * DC + c + 1)
                    nc.scalar.activation(h_t[:, c, cols], pair[:, c * 512:(c + 1) * 512], ACT.Identity,
                                         bias=mod_cols[:, first + c, b:b + 1],
                                         scale=mod_cols[:, first + 2 + c, b:b + 1]).then_inc(done, 1)

            def modulate_input(q):
                modulate(q, 0, slot_ps[:, q % 2, :], x_turned, h_ready)

            def values(q):
                for t in range(4):
                    act_e.wait_ge(rot_read, 4 * q + t + 1)
                    nc.scalar.copy(v_all[:, q // 2 * KV_HEADS:(q // 2 + 1) * KV_HEADS, q % 2 * 4 + t, 0:HD],
                                   unit_ps[:, t, QK:QKV].rearrange("p (g d) -> p g d", g=KV_HEADS)
                                   ).then_inc(v_read, 1)

            def hi_part(q):
                act_e.wait_ge(rot_sum, q + 1)
                nc.scalar.copy(parts_sb[:, q, 0, :], rot[:, q, :]).then_inc(p_hi, 1)

            def mid_part(q):
                act_e.wait_ge(p_rest, q + 1)
                nc.scalar.copy(parts_sb[:, q, 1, :], rot[:, q, :]).then_inc(p_mid, 1)

            def copy_keys(q):
                act_e.wait_ge(parts_dma[q % 2], PARTS_DMA)
                for fill, sets in ((3, 2), (4, 1)):
                    act_e.wait_ge(k_fill, q * 2 + fill - 2)
                    bank = fill_banks[q % 2][fill].bitcast(BF16)[KEY_ROW:P, 0:sets * 512]
                    nc.scalar.copy(parts_t[KEY_ROW:P, q % 2, 2 * fill:2 * fill + sets, :],
                                   bank.rearrange("p (s t) -> p s t", s=sets)).then_inc(k_out, 1)

            def copy_queries(q):
                if q >= 2:
                    act_e.wait_ge(parts_dma[q % 2], PARTS_DMA)
                for fill in range(3):
                    act_e.wait_ge(q_fill, q * 3 + fill + 1)
                    nc.scalar.copy(parts_t[:, q % 2, 2 * fill:2 * fill + 2, :],
                                   fill_banks[q % 2][fill].bitcast(BF16).rearrange("p (s t) -> p s t", s=2)
                                   ).then_inc(q_out[q % 2], 1)

            deviations(0, 1, ln_agg, ln_std)
            act_e.wait_ge(in_ident, 16)
            nc.scalar.copy(ident_bf[:], ident_sb[:]).then_inc(idents, 1)
            deviations(1, 1, ln_agg, ln_std)
            act_e.wait_ge(cols_mm, 1)
            nc.scalar.copy(mod_cols[:, 0:4, :].rearrange("p a b -> p (a b)"), out_ps[:, 0:8]).then_inc(cols_out, 1)
            act_e.wait_ge(cols_one, 1)
            modulate_input(0)
            modulate_input(1)
            deviations(2, 1, ln_agg, ln_std)
            deviations(3, 1, ln_agg, ln_std)
            act_e.wait_ge(v_ones, 1)
            values(0)
            modulate_input(2)
            hi_part(0)
            values(1)
            modulate_input(3)
            mid_part(0)
            hi_part(1)
            values(2)
            mid_part(1)
            hi_part(2)
            values(3)
            copy_queries(0)
            mid_part(2)
            hi_part(3)
            copy_queries(2)
            copy_keys(2)
            mid_part(3)

            def exps(group, step, lo, hi):
                first, n = STEPS[step][1], group.index
                for u in range(first + lo, first + hi):
                    user = u - P_RING
                    steps_before = sum(s[1] <= user % UNITS for s in STEPS)
                    if user >= 0:
                        act_e.wait_ge(pv_mm, n * 10 + steps_before)
                    elif not (isinstance(n, int) and n == 0):
                        act_e.wait_ge(pv_mm, n * 10 - 10 + steps_before)
                    act_e.wait_ge(unit_mm, n * UNITS + u + 1)
                    nc.scalar.activation(probs[:, u % P_RING, :], unit_ps[:, u % 3, :], ACT.Exp).then_inc(unit_exp, 1)

            def rows_copy(group, half):
                index = group.index * 2 + half
                act_e.wait_ge(rows_mm, index + 1)
                if not (isinstance(index, int) and index < 2):
                    act_e.wait_ge(rows_in, index * ROWS_IN - ROWS_IN)
                nc.scalar.copy(max_rows[:, half * HALF:(half + 1) * HALF],
                               slot_ps[0:MAX_PARTS * GROUP, ROWS[half] % 2, 0:512].bitcast(BF16)[:, 0:512]
                               ).then_inc(rows_out, 1)

            def out_copy(group, half):
                n = group.index
                act_e.wait_ge(pv_mm, n * 10 + LAST_STEP[half] + 1)
                if not (isinstance(n, int) and n == 0 and half == 0):
                    act_e.wait_ge(o_turned, n * 2 + half)
                nc.scalar.copy(o_t[:], out_ps).then_inc(o_copied, 1)

            def attend(group, first, last):
                exps(group, 0, 0, 4)
                if first:
                    exps(group, 1, 0, 4)
                    exps(group, 2, 0, 2)
                    rows_copy(group, 1)
                else:
                    out_copy(group.ahead(-1), 1)
                    rows_copy(group, 1)
                    exps(group, 1, 0, 4)
                    last_copies(last, 1)
                    exps(group, 2, 0, 2)
                    last_copies(last, 2)
                exps(group, 3, 0, 0)
                out_copy(group, 0)
                exps(group, 3, 0, 4)
                last_copies(last, 3)
                exps(group, 4, 0, 4)
                last_copies(last, 4)
                exps(group, 5, 0, 2)
                if not last:
                    rows_copy(group.ahead(1), 0)
                exps(group, 5, 2, 4)
                last_copies(last, 5)
                for step in range(6, 10):
                    exps(group, step, 0, STEPS[step][2])
                    last_copies(last, step)

            def last_copies(last, step):
                for what in LAST_COPIES[step] if last else ():
                    if what == "columns":
                        act_e.wait_ge(cols_mm, 2)
                        nc.scalar.copy(mod_cols[:, 4:8, :].rearrange("p a b -> p (a b)"), slot_ps[:, 0, 8:16]
                                       ).then_inc(cols_out, 1)
                    else:
                        copy_heads(what)

            def copy_heads(q):
                pair, cols = heads_pair[q], batch_and_cols(q)[1]
                for c in range(DC):
                    act_e.wait_ge(heads_mm, q * DC + c + 1)
                    if c == 0 and q >= 2:
                        act_e.wait_ge(wo_mm, (q - 2) * 4 + 4)
                    nc.scalar.copy(o_now_t[:, c, cols], pair[:, c * 512:(c + 1) * 512]).then_inc(heads_t, 1)

            rows_copy(Group(None, 0), 0)
            copy_queries(3)
            copy_keys(3)
            cycles(act_e, attend)
            out_copy(Group(None, NG - 1), 1)


            def hidden_tanh(q):
                act_e.wait_ge(hid_mm, q + 1)
                tiles = hidden_pair[q].rearrange("p (t e) -> p t e", t=4)
                nc.scalar.copy(logits[:, 4 * q:4 * q + 4, :], tiles[:, :, EI:EI + EXPERTS]).then_inc(hid_tanh, 1)
                nc.scalar.activation(hid_half[:, 4 * q:4 * q + 4, :], tiles[:, :, 0:EI], ACT.Tanh, scale=0.5
                                     ).then_inc(hid_tanh, 1)

            def router_exp(b):
                act_e.wait_ge(z_ready, b + 1)
                nc.scalar.activation(router_w[:, b * TT:(b + 1) * TT, :], pick[0][:], ACT.Exp).then_inc(z_exp, 1)

            def copy_acts(q):
                act_e.wait_ge(act_mm, q + 1)
                nc.scalar.copy(act_t[:, q % 2, :], acts_bank[q]).then_inc(act_out, 1)

            def modulate_sum(q):
                modulate(q, 4, sum_pair[q], e_turned, e_h)

            deviations(0, 2, e_agg, e_std)
            copy_heads(2)
            copy_heads(3)
            deviations(2, 1, e_agg, e_std)
            act_e.wait_ge(cols_one, 2)
            modulate_sum(0)
            deviations(3, 1, e_agg, e_std)
            modulate_sum(1)
            hidden_tanh(0)
            hidden_tanh(1)
            modulate_sum(2)
            router_exp(0)
            modulate_sum(3)
            hidden_tanh(2)
            hidden_tanh(3)
            copy_acts(0)
            copy_acts(1)
            router_exp(1)
            copy_acts(2)
            copy_acts(3)

        @block.gpsimd
        def _(pool):
            nc.gpsimd.memset(eps[:], EPS).then_inc(eps_set, 1)
            nc.gpsimd.memset(v_all[:], 0.0).then_inc(v_zero, 1)
            pool.wait_ge(v_zero, 1)
            nc.gpsimd.memset(v_all[:, :, :, HD:HD + 1], 1.0).then_inc(v_ones, 1)

            def add_products(q):
                pool.wait_ge(rot_read, 4 * q + 4)
                nc.gpsimd.tensor_tensor(rot[:, q, :], rot[:, q, :], rot_b[:, q % 2, :], ALU.add).then_inc(rot_sum, 1)

            def rest_of(q):
                pool.wait_ge(rot_sum, q + 1)
                pool.wait_ge(p_hi, q + 1)
                nc.gpsimd.tensor_tensor(rot[:, q, :], rot[:, q, :], parts_sb[:, q, 0, :], ALU.subtract
                                        ).then_inc(p_rest, 1)

            def lo_part(q):
                pool.wait_ge(p_mid, q + 1)
                pool.wait_ge(p_lo, q)
                nc.gpsimd.tensor_tensor(parts_sb[:, q, 2, :], rot[:, q, :], parts_sb[:, q, 1, :], ALU.subtract
                                        ).then_inc(p_lo, 1)

            for q in range(3):
                add_products(q)
            rest_of(2)
            add_products(3)
            lo_part(2)
            rest_of(3)
            lo_part(3)

            pool.wait_ge(v_ones, 1)
            pool.wait_ge(v_read, B * TT)
            for n in range(NG):
                if n >= NBUF:
                    pool.wait_ge(pv_mm, (n - NBUF) * 10 + 10)
                nc.gpsimd.tensor_copy(v_now[:, n % NBUF, :, :], v_all[:, n, :, :]).then_inc(v_here, 1)

            def gated_activations(q):
                pool.wait_ge(hid_read, q + 1)
                pool.wait_ge(chain_own, LINKS)
                quad = slice(4 * q, 4 * q + 4)
                gate = router_w[:, quad, :].rearrange("p t (e a) -> p (t e) a", a=1).to_broadcast(
                    [P, 4 * EXPERTS, INNER])
                nc.gpsimd.tensor_tensor(
                    act_now[:, quad, :].rearrange("p t (e i) -> p (t e) i", i=INNER),
                    act[:, quad, :].rearrange("p t (e i) -> p (t e) i", i=INNER), gate, ALU.mult
                ).then_inc(act_gated, 1)

            gated_activations(0)
            gated_activations(1)

        @block.vector
        def _(dve):
            dve.wait_ge(cond_e, 1)
            nc.vector.tensor_scalar(cond_exp[:], cond_exp[:], 1.0, None, ALU.add).then_inc(cond_s, 1)
            dve.wait_ge(cond_s, 1)
            nc.vector.reciprocal(cond_exp[:], cond_exp[:]).then_inc(cond_s, 1)
            dve.wait_ge(cond_s, 2)
            nc.vector.tensor_tensor(cond_silu[:], cond_sb[:], cond_exp[:], ALU.mult).then_inc(cond_r, 1)
            dve.wait_ge(cond_r, 1)
            for b in range(B):
                nc.vector.tensor_copy(cond_rep[:, :, b, :], cond_silu[:, :, b:b + 1].to_broadcast([P, DC, P])
                                      ).then_inc(cond_r, 1)

            def statistics(q, stat, agg):
                for t in range(4 * q, 4 * q + 4):
                    nc.vector.bn_stats(stats[:, t, :], x_sb[:, t, :]).then_inc(stat, 1)
                for t in range(4 * q, 4 * q + 4):
                    dve.wait_ge(stat, t + 1)
                    nc.vector.bn_aggr(mean_var[:, t, :], stats[:, t, :]).then_inc(agg, 1)

            def inverses(q, count, std_done, value, done):
                dve.wait_ge(std_done, value)
                tiles = slice(4 * q, 4 * (q + count))
                nc.vector.reciprocal(rstd[:, tiles], std[:, tiles]).then_inc(done, count)

            def normalised(q, inv, turned, done):
                dve.wait_ge(inv, q + 1)
                if q >= 2:
                    dve.wait_ge(turned, (q - 2) * DC + DC)
                for t in range(4):
                    tile = 4 * q + t
                    nc.vector.tensor_scalar(normed[:, q % 2 * 4 + t, :], x_sb[:, tile, :], mean_var[:, tile, 0:1],
                                            rstd[:, tile:tile + 1], ALU.subtract, ALU.mult).then_inc(done, 1)

            def first_statistics(q):
                dve.wait_ge(in_x[q], 16)
                statistics(q, ln_stat, ln_agg)

            def first_normalised(q):
                inverses(q, 1, ln_std, q + 1, ln_inv)
                normalised(q, ln_inv, x_turned, ln_x)

            def rotate(q, tiles=range(4)):
                if q >= 2:
                    dve.wait_ge(rot_sum, q - 1)
                heads = QK // HD
                for t in tiles:
                    own = slice(t * QK, (t + 1) * QK)
                    a = rot[:, q, own].rearrange("p (s e) -> p s e", e=HD // 2)
                    b4 = rot_b[:, q % 2, own].rearrange("p (h w e) -> p h w e", w=2, e=HD // 2)
                    proj = unit_ps[:, t, 0:QK]
                    halves = proj.rearrange("p (h w e) -> p h w e", w=2, e=HD // 2)

                    def table(j, count):
                        return rope_sb[:, q % 2 * 4 + t, j:j + 1, :].to_broadcast([P, count, HD // 2])

                    dve.wait_ge(qkv_mm, 4 * q + t + 1)
                    nc.vector.tensor_tensor(a, proj.rearrange("p (s e) -> p s e", e=HD // 2), table(0, 2 * heads),
                                            ALU.mult)
                    nc.vector.tensor_tensor(b4[:, :, 0, :], halves[:, :, 1, :], table(1, heads), ALU.mult)
                    nc.vector.tensor_tensor(b4[:, :, 1, :], halves[:, :, 0, :], table(2, heads), ALU.mult
                                            ).then_inc(rot_read, 1)

            def rest_of(q):
                dve.wait_ge(p_hi, q + 1)
                nc.vector.tensor_tensor(rot[:, q, :], rot[:, q, :], parts_sb[:, q, 0, :], ALU.subtract
                                        ).then_inc(p_rest, 1)

            def lo_part(q):
                dve.wait_ge(p_mid, q + 1)
                nc.vector.tensor_tensor(parts_sb[:, q, 2, :], rot[:, q, :], parts_sb[:, q, 1, :], ALU.subtract
                                        ).then_inc(p_lo, 1)

            def copy_keys(q):
                if q >= 2:
                    dve.wait_ge(parts_dma[q % 2], PARTS_DMA)
                for fill, sets in ((3, 2), (4, 1)):
                    dve.wait_ge(k_fill, q * 2 + fill - 2)
                    bank = fill_banks[q % 2][fill].bitcast(BF16)[KEY_ROW:P, 0:sets * 512]
                    nc.vector.tensor_copy(parts_t[KEY_ROW:P, q % 2, 2 * fill:2 * fill + sets, :],
                                          bank.rearrange("p (s t) -> p s t", s=sets)).then_inc(k_out, 1)

            def copy_queries(q):
                for fill in range(3):
                    dve.wait_ge(q_fill, q * 3 + fill + 1)
                    nc.vector.tensor_copy(parts_t[:, q % 2, 2 * fill:2 * fill + 2, :],
                                          fill_banks[q % 2][fill].bitcast(BF16).rearrange("p (s t) -> p s t", s=2)
                                          ).then_inc(q_out[q % 2], 1)

            first_statistics(0)
            first_normalised(0)
            first_statistics(1)
            first_normalised(1)
            dve.wait_ge(cols_out, 1)
            nc.vector.tensor_scalar(mod_cols[:, 2:4, :], mod_cols[:, 2:4, :], 1.0, None, ALU.add).then_inc(cols_one, 1)
            first_statistics(2)
            first_statistics(3)
            first_normalised(2)
            dve.wait_ge(in_w, 16 * 2)
            rotate(0)
            first_normalised(3)
            rotate(1)
            rest_of(0)
            rotate(2)
            lo_part(0)
            rest_of(1)
            rotate(3, (0,))
            lo_part(1)
            rotate(3, (1, 2, 3))
            copy_keys(0)
            copy_queries(1)
            copy_keys(1)

            def take_max(group, where):
                kind, slot = RING[where]
                if kind == "rows":
                    return
                tile, head, heads = SLOTS[slot]
                keys = (tile + 1) * P
                dve.wait_ge(slot_mm, group.index * NSLOTS + slot + 1)
                src = slot_ps[:, where % 2, :].rearrange("p (j k) -> p j k", j=heads)[:, :, 0:keys]
                nc.vector.tensor_reduce(neg_max[:, tile, head:head + heads], src, AX.X, ALU.max, negate=True
                                        ).then_inc(slot_max, 1)

            def split_max(group, half):
                tiles = slice(4 * half, 4 * half + 4)
                n = group.index
                dve.wait_ge(slot_max, n * NSLOTS + (NSLOTS if half else SLOTS_LOW))
                if not (isinstance(n, int) and n == 0):
                    dve.wait_ge(rows_mm, n * 2 + half - 1)
                nc.vector.tensor_copy(max_parts[:, tiles, :, 0], neg_max[:, tiles, :]).then_inc(hi_own, 1)
                dve.wait_ge(hi_own, n * 2 + half + 1)
                nc.vector.tensor_tensor(max_parts[:, tiles, :, 1], neg_max[:, tiles, :],
                                        max_parts[:, tiles, :, 0], ALU.subtract).then_inc(max_split, 1)

            def normalise(group, half):
                n = group.index
                bank = out_ps.rearrange("p (t h c) -> p t h c", t=4, h=GROUP)
                dve.wait_ge(o_turned, n * 2 + half + 1)
                nc.vector.reciprocal(inv_sum[:], bank[:, :, :, HD]).then_inc(o_inv, 1)
                dve.wait_ge(o_inv, n * 2 + half + 1)
                dst = heads_out[:, 4 * half:4 * half + 4, n, :].rearrange("p t (h c) -> p t h c", c=HD)
                nc.vector.tensor_tensor(
                    dst, bank[:, :, :, 0:HD],
                    inv_sum[:].rearrange("p t (h a) -> p t h a", a=1).to_broadcast([P, 4, GROUP, HD]),
                    ALU.mult).then_inc(o_normed, 1)

            def make_gates():
                dve.wait_ge(gates_mm, 4)
                both = slot_ps[:, 1, :].rearrange("p (j d) -> p j d", j=4)
                nc.vector.tensor_scalar(gate_abs[:], both, -1.0, 0.25, ALU.mult, ALU.max).then_inc(gates_own, 1)
                nc.vector.tensor_scalar(gates[:], both, 0.0, 2.0, ALU.is_ge, ALU.mult).then_inc(gates_own, 1)
                dve.wait_ge(gates_own, 2)
                nc.vector.tensor_tensor(gate_abs[:], both, gate_abs[:], ALU.max).then_inc(gates_own, 1)
                dve.wait_ge(gates_own, 3)
                nc.vector.scalar_tensor_tensor(gates[:], gates[:], -1.0, gate_abs[:], ALU.add, ALU.mult
                                               ).then_inc(gates_own, 1)

            def fold_gates():
                dve.wait_ge(in_late, 16 * 5)
                dve.wait_ge(gates_own, 4)
                for b in range(B):
                    gate = gates[:, b:b + 1, :].to_broadcast([P, DC, D])
                    nc.vector.tensor_tensor(wo_gated[:, b, :, :], wo_sb[:], gate, ALU.mult).then_inc(gated, 1)
                for b in range(B):
                    nc.vector.scalar_tensor_tensor(up_gated[:, b, :], up_sb[:], 0.5, gates[:, 2 + b, :],
                                                   ALU.mult, ALU.mult).then_inc(gated, 1)

            def add_output(q):
                dve.wait_ge(wo_mm, 4 * q + 4)
                pair, here = output_pair[q], x_sb[:, 4 * q:4 * q + 4, :]
                nc.vector.tensor_tensor(here, pair.rearrange("p (t d) -> p t d", t=4), here, ALU.add).then_inc(x_sum, 1)
                dve.wait_ge(x_sum, q + 1)
                statistics(q, e_stat, e_agg)

            def attend(group, first, last):
                before, ahead = group.ahead(-1), group.ahead(1)
                if first:
                    for step in FIRST_OWN:
                        for w in step:
                            take_max(group, w)
                    split_max(group, 1)
                elif last:
                    normalise(before, 1)
                    make_gates()
                    normalise(group, 0)
                    fold_gates()
                    dve.wait_ge(cols_out, 2)
                    nc.vector.tensor_scalar(mod_cols[:, 6:8, :], mod_cols[:, 6:8, :], 1.0, None, ALU.add
                                            ).then_inc(cols_one, 1)
                    for q in range(2):
                        add_output(q)
                    return
                for w in range(len(RING)):
                    if w == BEFORE_AT and not first:
                        normalise(before, 1)
                    if w == SLOTS_LOW:
                        split_max(ahead, 0)
                    if w == (FIRST_AT if first else OWN_AT):
                        normalise(group, 0)
                    take_max(ahead, w)
                split_max(ahead, 1)

            for w in range(SLOTS_LOW):
                take_max(Group(None, 0), w)
            split_max(Group(None, 0), 0)
            for w in OPENING[SLOTS_LOW:]:
                take_max(Group(None, 0), w)
            cycles(dve, attend)
            normalise(Group(None, NG - 1), 1)


            def activations(q):
                quad = slice(4 * q, 4 * q + 4)
                tiles = hidden_pair[q].rearrange("p (t e) -> p t e", t=4)
                dve.wait_ge(hid_tanh, q * 2 + 2)
                nc.vector.scalar_tensor_tensor(act[:, quad, :], hid_half[:, quad, :], 1.0, tiles[:, :, 0:EI],
                                               ALU.add, ALU.mult).then_inc(hid_read, 1)

            inverses(0, 2, e_std, 1, e_inv)
            normalised(0, e_inv, e_turned, e_x)
            normalised(1, e_inv, e_turned, e_x)
            add_output(2)
            add_output(3)
            for q in (2, 3):
                inverses(q, 1, e_std, q, e_inv)
                normalised(q, e_inv, e_turned, e_x)
            EXPERT_ROW = [P, TT, EXPERTS]
            ranks = rank_sb[:].rearrange("p (a e) -> p a e", a=1).to_broadcast(EXPERT_ROW)

            def expert_gates(b):
                links = [b * LINKS]
                tiles = slice(b * TT, (b + 1) * TT)
                weights = router_w[:, tiles, :]

                def link(ins):
                    links[0] += 1
                    ins.then_inc(chain_own, 1)
                    dve.wait_ge(chain_own, links[0])

                def row(j):
                    return row_stat[:, j:j + 1, :].rearrange("p a t -> p t a").to_broadcast(EXPERT_ROW)

                def reduce(j, src, op):
                    link(nc.vector.tensor_reduce(row_stat[:, j, :], src, AX.X, op))

                dve.wait_ge(hid_tanh, (b + 1) * 4)
                reduce(0, logits[:, tiles, :], ALU.max)
                nc.vector.tensor_tensor(pick[0][:], logits[:, tiles, :], row(0), ALU.subtract).then_inc(z_ready, 1)
                dve.wait_ge(z_exp, b + 1)
                reduce(1, weights, ALU.add)
                link(nc.vector.reciprocal(row_stat[:, 2, :], row_stat[:, 1, :]))
                link(nc.vector.tensor_tensor(weights, weights, row(2), ALU.mult))
                reduce(3, weights, ALU.max)
                link(nc.vector.tensor_tensor(pick[0][:], weights, row(3), ALU.is_ge))
                link(nc.vector.tensor_tensor(pick[0][:], pick[0][:], ranks, ALU.mult))
                reduce(4, pick[0][:], ALU.max)
                link(nc.vector.tensor_tensor(pick[1][:], pick[0][:], row(4), ALU.is_equal))
                link(nc.vector.scalar_tensor_tensor(pick[2][:], pick[1][:], -2.0, weights, ALU.mult, ALU.add))
                reduce(5, pick[2][:], ALU.max)
                link(nc.vector.tensor_tensor(pick[3][:], pick[2][:], row(5), ALU.is_ge))
                link(nc.vector.tensor_tensor(pick[3][:], pick[3][:], ranks, ALU.mult))
                reduce(0, pick[3][:], ALU.max)
                link(nc.vector.tensor_tensor(pick[4][:], pick[3][:], row(0), ALU.is_equal))
                link(nc.vector.tensor_tensor(pick[1][:], pick[1][:], pick[4][:], ALU.add))
                link(nc.vector.tensor_tensor(weights, weights, pick[1][:], ALU.mult))
                assert links[0] == (b + 1) * LINKS, links

            def gated_activations(q):
                dve.wait_ge(hid_read, q + 1)
                dve.wait_ge(act_gated, q)
                quad = slice(4 * q, 4 * q + 4)
                gate = router_w[:, quad, :].rearrange("p t (e a) -> p (t e) a", a=1).to_broadcast(
                    [P, 4 * EXPERTS, INNER])
                nc.vector.tensor_tensor(
                    act_now[:, quad, :].rearrange("p t (e i) -> p (t e) i", i=INNER),
                    act[:, quad, :].rearrange("p t (e i) -> p (t e) i", i=INNER), gate, ALU.mult
                ).then_inc(act_gated, 1)

            activations(0)
            activations(1)
            expert_gates(0)
            activations(2)
            activations(3)
            expert_gates(1)
            gated_activations(2)
            gated_activations(3)
            for q in range(QUADS):
                for half in range(2):
                    dve.wait_ge(up_mm, q * 2 + half + 1)
                    here = x_sb[:, 4 * q + 2 * half:4 * q + 2 * half + 2, :]
                    bank = experts_pair[q][:, half * 512:(half + 1) * 512]
                    nc.vector.tensor_tensor(here, bank.rearrange("p (t d) -> p t d", t=2), here, ALU.add
                                            ).then_inc(y_sum, 1)


def constants():
    bf = mybir.dt.np(BF16)
    half = HD // 2
    theta = (1.0 / np.float32(10000.0) ** (np.arange(half, dtype=np.float32) / np.float32(half))).astype(np.float32)
    freqs = np.outer(np.arange(T, dtype=np.float32), theta).astype(np.float32)
    cos, sin = np.cos(freqs), np.sin(freqs)
    scale = np.float32(HD ** -0.25)
    table = np.stack([cos * scale, -sin * scale, sin * scale], axis=1).astype(np.float32)
    rope = np.ascontiguousarray(table.reshape(TT, P, 3, half).transpose(1, 0, 2, 3))

    slopes = np.power(np.float32(2.0), -8.0 * np.arange(1, HEADS + 1, dtype=np.float32) / HEADS).astype(np.float32)
    parts, left = [], slopes.copy()
    for _ in range(3):
        part = left.astype(bf).astype(np.float32)
        parts.append(part)
        left = left - part
    pos = np.arange(T)
    q_tile, k_tile, k_in = pos // P, pos // P * P, pos % P
    q_const = np.zeros((HEADS, FEATURE_ROW, T), np.float32)
    k_const = np.zeros((FEATURE_ROW, T), np.float32)
    k_const[0:MAX_PARTS] = 1.0
    r = MAX_PARTS
    for part in parts:
        q_const[:, r] = part[:, None]
        k_const[r] = k_tile
        r += 1
        for bit in (4, 2, 1):
            q_const[:, r] = -part[:, None] * (bit * P) * ((q_tile // bit) % 2)
            k_const[r] = 1.0
            r += 1
    for part in parts:
        q_const[:, r] = part[:, None]
        k_const[r] = k_in
        r += 1
    assert r <= FEATURE_ROW
    q_const = q_const.reshape(KV_HEADS, GROUP, FEATURE_ROW, T).transpose(0, 2, 1, 3)
    q_const = np.ascontiguousarray(np.concatenate([q_const] * B)).astype(bf)
    causal = np.where(np.arange(P)[None, :] > np.arange(P)[:, None], np.float32(MASKED), np.float32(0))
    causal = np.stack([causal, causal.T]).astype(bf)
    rank = np.ascontiguousarray(np.broadcast_to(np.arange(EXPERTS, 0, -1, dtype=np.float32), (P, EXPERTS)))
    return {"rope": rope, "q_const": q_const, "k_const": k_const.astype(bf), "causal": causal,
            "ident": np.eye(P, dtype=np.float32), "rank": rank}


def kernel(**inputs):
    import concourse.bacc as bacc
    from concourse.bass_utils import run_bass_kernel_spmd

    a = {k: np.asarray(v) for k, v in inputs.items()}
    down = a["L0_ffn_down_w"].transpose(2, 0, 1).reshape(D, EI)
    arrays = {
        "x": a["L0_attn_x"],
        "w_qkv": np.concatenate([a["L0_attn_Wq"], a["L0_attn_Wk"], a["L0_attn_Wv"]], axis=1),
        "w_out": a["L0_attn_Wo"],
        "w_hidden_router": np.concatenate([down, a["L0_ffn_router_w"].T], axis=1),
        "w_up": a["L0_ffn_up_w"].transpose(0, 2, 1).reshape(EI, D),
        "cond_t": a["L0_c"].T,
        "w_mod": a["L0_wmod"],
        **constants(),
    }
    arrays = {k: np.ascontiguousarray(v) for k, v in arrays.items()}
    nc = bacc.Bacc("TRN2", target_bir_lowering=False, num_devices=1)
    args = [nc.dram_tensor(f"in_{k}", v.shape, mybir.dt.from_np(v.dtype), kind="ExternalInput").ap()
            for k, v in arrays.items()]
    out = nc.dram_tensor("out_y", (B, T, D), F32, kind="ExternalOutput").ap()
    adaln_block(nc, *args, out)
    r = run_bass_kernel_spmd(nc, [{f"in_{k}": v for k, v in arrays.items()}], core_ids=[0])
    return r.results[0]["out_y"]
```
